# Optimizing a Trainium2 kernel written in Bass

```python
import numpy as np
import jax
import jax.numpy as jnp

def _softmax(x, axis=-1):
    return jax.nn.softmax(x, axis=axis)
def _gelu(x):
    return jax.nn.gelu(x, approximate=True)
def _silu(x):
    return jax.nn.silu(x)
def _sigmoid(x):
    return jax.nn.sigmoid(x)
def _layernorm(x, axis=-1, eps=1e-5):
    m = jnp.mean(x, axis=axis, keepdims=True)
    v = jnp.var(x, axis=axis, keepdims=True)
    return (x - m) / jnp.sqrt(v + eps)
def _scatter_add(tgt, idx, src, axis=0):
    return tgt.at[idx].add(src)
def _segment_sum(src, seg, n):
    return jax.ops.segment_sum(src, seg, n)

kernel_name = 'mk_conv_preact_d2_conv_nchw256_746050'

def setup_inputs(seed: int = 0):
    np.random.seed(seed)
    _w = jnp.asarray
    def _rec_inputs():
        import jax
        import jax.numpy as jnp
        _gk = jax.random.key(seed)
        x = -0.000125 + 0.9999 * jax.random.normal(jax.random.fold_in(_gk, 1), (8, 256, 128, 128), jnp.float32)
        return x
    x = _rec_inputs()
    def _L0_conv_setup():
        import jax, jax.numpy as jnp
        import numpy as np
        FC, FH, FW, CS = (8, 2, 2, 8)
        key = jax.random.key(seed)
        ks = jax.random.split(key, 6)
        n, c, h, w = (8, 256, 128, 128)
        hd = 256
        return {'x': jax.random.normal(ks[0], (n, c, h, w), dtype=jnp.float32), 'Wp': jax.random.normal(ks[1], (2 * hd, c), dtype=jnp.float32) * 0.05, 'bp': jax.random.normal(ks[2], (2 * hd,), dtype=jnp.float32) * 0.05, 'Wm': jax.random.normal(ks[3], (c, hd), dtype=jnp.float32) * 0.05, 'bm': jax.random.normal(ks[4], (c,), dtype=jnp.float32) * 0.05, 'alpha': jnp.ones((1,), jnp.float32), 'beta': jnp.zeros((1,), jnp.float32)}
    _L0_conv_all = _L0_conv_setup()
    _L0_conv_in = {k: v for k, v in _L0_conv_all.items() if k in ('Wp', 'bp', 'Wm', 'bm', 'alpha', 'beta', )}
    del _L0_conv_all

    def _L1_conv_setup():
        import jax, jax.numpy as jnp
        import numpy as np
        import math
        DCT_H = 64
        DCT_W = 64
        CHANNEL = 256
        REDUCTION = 16

        def _dct_basis(L, POS):
            f = np.arange(L)[:, None].astype(np.float64)
            p = np.arange(POS)[None, :].astype(np.float64)
            b = np.cos(np.pi * f * (p + 0.5) / POS) / math.sqrt(POS)
            b[1:] *= math.sqrt(2.0)
            return b

        def _dct_filters(h, w):
            L = h
            bh = _dct_basis(L, h)
            bw = _dct_basis(L, w)
            filt = np.einsum('lh,lw->lhw', bh, bw)
            return jnp.asarray(filt, dtype=jnp.float32)
        key = jax.random.key(seed)
        k1, k2, k3 = jax.random.split(key, 3)
        N, C, H, W = (32, CHANNEL, DCT_H, DCT_W)
        Cr = C // REDUCTION
        x = jax.random.normal(k1, (N, C, H, W), dtype=jnp.float32)
        w1 = jax.random.normal(k2, (Cr, C), dtype=jnp.float32) * (1.0 / math.sqrt(C))
        w2 = jax.random.normal(k3, (C, Cr), dtype=jnp.float32) * (1.0 / math.sqrt(Cr))
        return {'x': x, 'w1': w1, 'w2': w2}
    _L1_conv_all = _L1_conv_setup()
    _L1_conv_in = {k: v for k, v in _L1_conv_all.items() if k in ('w1', 'w2', )}
    del _L1_conv_all

    return {
        "x": x,
        "L0_conv_Wp": _L0_conv_in["Wp"],
        "L0_conv_bp": _L0_conv_in["bp"],
        "L0_conv_Wm": _L0_conv_in["Wm"],
        "L0_conv_bm": _L0_conv_in["bm"],
        "L0_conv_alpha": _L0_conv_in["alpha"],
        "L0_conv_beta": _L0_conv_in["beta"],
        "L1_conv_w1": _L1_conv_in["w1"],
        "L1_conv_w2": _L1_conv_in["w2"],
    }

def reference(x, L0_conv_Wp, L0_conv_bp, L0_conv_Wm, L0_conv_bm, L0_conv_alpha, L0_conv_beta, L1_conv_w1, L1_conv_w2):
    import jax
    import jax.numpy as jnp
    def _L0_conv_ref(x, Wp, bp, Wm, bm, alpha, beta):
        import jax, jax.numpy as jnp
        import numpy as np
        FC, FH, FW, CS = (8, 2, 2, 8)
        fc, fh, fw, cs = (FC, FH, FW, CS)
        n, c, h, w = x.shape
        sh, sw = (h // fh, w // fw)
        m, l, s = (n * fc * fh * fw, sh * sw, cs * cs)
        y = jnp.einsum('nchw,dc->ndhw', x, Wp) + bp[None, :, None, None]
        sc = y.shape[1] // fc
        y = y.reshape(n, fc, sc, fh, sh, fw, sw).transpose(0, 1, 3, 5, 2, 4, 6)
        y = y.reshape(m, sc, sh, sw)
        center = y.reshape(m, sc, cs, sh // cs, cs, sw // cs).mean(axis=(3, 5))
        xf = y.reshape(m, sc, l).transpose(0, 2, 1)
        cf = center.reshape(m, sc, s).transpose(0, 2, 1)
        scv = sc // 2
        x_point, x_value = (xf[..., :scv], xf[..., scv:])
        c_point, c_value = (cf[..., :scv], cf[..., scv:])
        nx = x_point / jnp.maximum(jnp.linalg.norm(x_point, axis=2, keepdims=True), 1e-12)
        nc = c_point / jnp.maximum(jnp.linalg.norm(c_point, axis=2, keepdims=True), 1e-12)
        sim = jnp.einsum('mlc,msc->mls', nx, nc)
        sim = jax.nn.sigmoid(alpha * sim + beta)
        max_v = sim.max(axis=2)
        max_i = sim.argmax(axis=2)
        idx = (max_i + s * jnp.arange(m)[:, None]).reshape(-1)
        mv = max_v.reshape(-1)
        xv = x_value.reshape(m * l, scv)
        cv = c_value.reshape(m * s, scv)
        cat_x = jnp.concatenate([xv, jnp.ones((m * l, 1), y.dtype)], axis=1)
        cat_c = jnp.concatenate([cv, jnp.ones((m * s, 1), y.dtype)], axis=1)
        agg = cat_c.at[idx].add(mv[:, None] * cat_x)
        agg = agg[:, :-1] / agg[:, -1:]
        disp = mv[:, None] * agg[idx]
        disp = disp.reshape(n, fc, fh, fw, sh, sw, scv).transpose(0, 1, 6, 2, 4, 3, 5)
        disp = disp.reshape(n, fc * scv, h, w)
        out = jnp.einsum('nchw,dc->ndhw', disp, Wm) + bm[None, :, None, None]
        return out

    def _L1_conv_ref(x, w1, w2):
        import jax, jax.numpy as jnp
        import numpy as np
        import math
        DCT_H = 64
        DCT_W = 64
        CHANNEL = 256
        REDUCTION = 16

        def _dct_basis(L, POS):
            f = np.arange(L)[:, None].astype(np.float64)
            p = np.arange(POS)[None, :].astype(np.float64)
            b = np.cos(np.pi * f * (p + 0.5) / POS) / math.sqrt(POS)
            b[1:] *= math.sqrt(2.0)
            return b

        def _dct_filters(h, w):
            L = h
            bh = _dct_basis(L, h)
            bw = _dct_basis(L, w)
            filt = np.einsum('lh,lw->lhw', bh, bw)
            return jnp.asarray(filt, dtype=jnp.float32)
        N, C, H, W = x.shape
        filt = _dct_filters(H, W)
        freq = jnp.einsum('nchw,lhw->ncl', x, filt)
        y = jnp.mean(freq, axis=2)
        h = jax.nn.relu(y @ w1.T)
        s = jax.nn.sigmoid(h @ w2.T)
        return x * s[:, :, None, None]

    def _gn(v, G=32, eps=1e-5):
        B_, C_, H_, W_ = v.shape
        g = v.reshape(B_, G, C_ // G, H_, W_)
        m = jnp.mean(g, axis=(2, 3, 4), keepdims=True)
        s = jnp.var(g, axis=(2, 3, 4), keepdims=True)
        return ((g - m) / jnp.sqrt(s + eps)).reshape(v.shape)

    def _ln_c(v, eps=1e-6):
        m = jnp.mean(v, axis=1, keepdims=True)
        s = jnp.var(v, axis=1, keepdims=True)
        return (v - m) / jnp.sqrt(s + eps)

    def _ln_t(v, eps=1e-5):
        m = jnp.mean(v, axis=-1, keepdims=True)
        s = jnp.var(v, axis=-1, keepdims=True)
        return (v - m) / jnp.sqrt(s + eps)

    def _to_tokens(v):
        B_, C_, H_, W_ = v.shape
        return v.reshape(B_, C_, H_ * W_).transpose(0, 2, 1)
    def _from_tokens(t, like):
        B_, C_, H_, W_ = like.shape
        return t.transpose(0, 2, 1).reshape(B_, C_, H_, W_)

    x = x + _L0_conv_ref(_gn(x), L0_conv_Wp, L0_conv_bp, L0_conv_Wm, L0_conv_bm, L0_conv_alpha, L0_conv_beta)
    x = x + _L1_conv_ref(_gn(x), L1_conv_w1, L1_conv_w2)
    return x


_drawn_inputs = setup_inputs


def setup_inputs(seed=0):
    import zlib

    import numpy as np

    out = dict(_drawn_inputs(seed))
    spreads = {}
    factors = {'L1_conv_w1': 4.734, 'L1_conv_w2': 4.346}
    for name, (base, spread) in spreads.items():
        noise = np.random.default_rng([zlib.crc32(name.encode()), seed]).standard_normal(out[name].shape)
        drawn = base * np.exp(spread * noise) if base else spread * noise
        out[name] = jnp.asarray(drawn.astype(out[name].dtype))
    for name, factor in factors.items():
        out[name] = (out[name] * factor).astype(out[name].dtype)
    return out
```

```python
from contextlib import ExitStack

import concourse.bass as bass
from concourse import mybir

F32 = mybir.dt.float32
F32R = mybir.dt.float32r
BF16 = mybir.dt.bfloat16
U8 = mybir.dt.uint8
ALU = mybir.AluOpType
ACT = mybir.ActivationFunctionType
AX = mybir.AxisListType

P = 128
HEADS = 8
CH = 32
CENTRES = 64
CS = 8
EPS = 1e-5
NORM2_MIN = 1e-24
LN_SCALE = 2.0 ** 20
LN2 = 0.6931471805599453

CREDIT = 2


def done(group):
    return group + 1 + CREDIT


def free(group):
    return group + 1


def before(group):
    return group + CREDIT


def cluster_block(nc, x, wp_t, bp_col, bv_diag, wm_t, bm_col, alpha, beta, w1_t, w2_t, first_centre, out):
    N, C, H, W = x.shape
    K = C // P
    RH, RW = H // 2, W // 2
    ROWS = 4
    PX = ROWS * RW
    TILES = PX // P
    GROUPS = RH // ROWS
    PAIRS = GROUPS // 2
    KT = HEADS // 2
    HS = HEADS * CENTRES
    M = HEADS * CH // P
    HPM = HEADS // M
    UNIT = CS * W
    UNITS = H // CS
    AGG = 2 * (CH + 1)
    HIDDEN = w1_t.shape[1]

    xf = x.rearrange("n (k p) h w -> n p k (h w)", p=P)
    of = out.rearrange("n (k p) h w -> n p k (h w)", p=P)

    ctx = ExitStack()
    with ctx:
        def sb(name, shape, dt=F32):
            return ctx.enter_context(nc.sbuf_tensor(name, shape, dt))

        def sem(name):
            return ctx.enter_context(nc.semaphore(name))

        img = sb("img", [P, K, H, W])
        hot_t = sb("hot_t", [P, GROUPS, KT * PX], U8)
        mv = sb("mv", [P, GROUPS * TILES, HEADS])
        xh = sb("xh", [P, 2, K, PX], F32R)
        xl = sb("xl", [P, 2, K, PX], F32R)
        yh = sb("yh", [P, M, PX], F32R)
        yl = sb("yl", [P, M, PX], F32R)
        sq = sb("sq", [P, 2, M, PX])
        hot = sb("hot", [P, 2, TILES, HS], BF16)
        work = sb("work", [P, 2640], BF16)
        vals = work[:, 0:1056].bitcast(F32).rearrange("p (t h c) -> p t h c", t=TILES, h=HEADS)
        vpart = [work[:, 1056 + 528 * s:1584 + 528 * s].rearrange("p (t h c) -> p t h c", t=TILES, h=HEADS)
                 for s in range(3)]
        hot_s = work[:, 0:2 * KT * PX].rearrange("p (b f) -> p b f", b=2)
        gath = [hot[:, b, :, :].rearrange("p t f -> p (t f)").bitcast(F32) for b in range(2)]
        newton = work[:, 0:1024].bitcast(F32)
        rank = sb("rank", [P, 2, TILES, HEADS])
        rnorm = sb("rnorm", [P, 2, TILES * HEADS])
        lnn = sb("lnn", [P, TILES * HEADS])
        zero = sb("zero", [P, KT * AGG], BF16)
        zarg = sb("zarg", [P, 2, TILES * HEADS])
        ez = sb("ez", [P, TILES * HEADS])
        wph = sb("wph", [P, K, 2 * C], F32R)
        wpl = sb("wpl", [P, K, 2 * C], F32R)
        wmh = sb("wmh", [P, M, C], F32R)
        wml = sb("wml", [P, M, C], F32R)
        ch = sb("ch", [P, M, HPM * CENTRES], F32R)
        cl = sb("cl", [P, M, HPM * CENTRES], F32R)
        tab = sb("tab", [P, 3, KT, 2, CH], BF16)
        aggf = sb("aggf", [P, KT, CH])
        aggr = sb("aggr", [P, KT, CH])
        den = sb("den", [P, KT, 1])
        chunk = sb("chunk", [P, UNIT])
        pooled = sb("pooled", [P, K, UNITS, UNITS])
        st = sb("st", [P, K, UNITS * 2, 6])
        st1 = sb("st1", [P, M, GROUPS, 6])
        agg1 = sb("agg1", [P, 4, M, 2])
        cen = sb("cen", [P, M, UNITS * UNITS])
        cvd = sb("cvd", [P, 4, KT, CH])
        bvd0 = sb("bvd0", [P, KT, CH])
        bvd = sb("bvd", [P, KT, CH])
        ident = sb("ident", [P, P])
        identb = sb("identb", [P, P], BF16)
        gsum = sb("gsum", [P, P])
        small = sb("small", [P, 64])
        hsum = sb("hsum", [P, HPM, CH])
        pair = sb("pair", [P, M, 2])
        e2 = sb("e2", [P, 4, M])
        w1s = sb("w1s", [P, K, HIDDEN])
        w2s = sb("w2s", [HIDDEN, C])
        cols = sb("cols", [P, 16])
        bp_s, bm_s = cols[:, 0:2], cols[:, 2:4]
        alpha_s, beta_s, s0_s, keep_s = cols[:, 4:5], cols[:, 5:6], cols[:, 6:7], cols[:, 7:8]
        bpf = cols[:, 8:10]
        nbeta = cols[:, 10:11]
        lnbias = cols[:, 11:12]

        raw = sq[:, :, :, :].rearrange("p a m f -> p (a m f)").rearrange("p (k d) -> p k d", k=K)

        bank = [ctx.enter_context(nc.psum_tensor(f"bank{i}", [P, 512], F32)) for i in range(8)]
        y_ps = [bank[i][:, :].rearrange("p (m f) -> p m f", m=M) for i in range(2)]
        s_ps = [bank[2], bank[3]]
        v_ps = bank[4][:, :].rearrange("p (t h c) -> p t h c", t=TILES, h=HEADS)
        t_ps = bank[5][:, :].bitcast(BF16).rearrange("p (k f) -> p k f", k=KT)
        a_ps = bank[6][:, 0:KT * AGG].rearrange("p (k c) -> p k c", k=KT)
        n_ps = bank[7]
        g_ps = [bank[0], bank[1]]
        d_ps = [bank[4][:, :].rearrange("p (m f) -> p m f", m=M), bank[5][:, :].rearrange("p (m f) -> p m f", m=M)]
        o_ps = [bank[2][:, :].rearrange("p (m f) -> p m f", m=M), bank[3][:, :].rearrange("p (m f) -> p m f", m=M)]

        diagonal = img[:, :, :, :].rearrange("p k h w -> p k (h w)")[:, :, 0:H * W:W + 1]

        s_const = sem("const_loaded")
        s_zero = sem("cleared")
        s_ident = sem("identity_ready")
        s_wm = sem("mix_weights_split")
        s_img = sem("image_loaded")
        s_chunk = sem("chunk_loaded")
        s_chunk_used = sem("chunk_used")
        s_raw = sem("weights_loaded")
        s_raw_free = sem("weights_place_free")
        s_stat = sem("statistics_ready")
        s_gst = sem("group_statistics_summed")
        s_fold = sem("weights_folded")
        s_wph = sem("folded_high")
        s_wpl = sem("folded_low")
        s_cen = sem("centres_projected")
        s_cenq = sem("centres_squared")
        s_cenn = sem("centres_norms")
        s_cv = sem("centre_values")
        s_cvd = sem("centre_values_taken")
        s_ln = sem("logs")
        s_lnreq = sem("log_asked")
        s_c = sem("region_centres_ready")
        s_xh = sem("x_high")
        s_xl = sem("x_low")
        s_yp = sem("projected")
        s_yh = sem("y_high")
        s_sq = sem("squared")
        s_yl = sem("y_low")
        s_sim = [sem("similar0"), sem("similar1")]
        s_hot = [sem("one_hot0"), sem("one_hot1")]
        s_v = sem("values")
        s_vs = sem("values_scaled")
        s_n2 = sem("norms")
        s_nc = sem("norms_guarded")
        s_rn = sem("norms_inverted")
        s_z = sem("argument")
        s_ez = sem("exponential")
        s_t = sem("transposed")
        s_te = sem("transposed_kept")
        s_v1 = sem("values_part1")
        s_r1 = sem("values_rest1")
        s_v2 = sem("values_part2")
        s_v3 = sem("values_part3")
        s_agg = sem("aggregated")
        s_sum = sem("region_summed")
        s_tab = sem("region_table_ready")
        s_hs = sem("hot_widened")
        s_g = sem("gathered")
        s_d = sem("weighted")
        s_dt = sem("weighted_transposed")
        s_dh = sem("weighted_high")
        s_dl = sem("weighted_low")
        s_o = sem("mixed")
        s_res = sem("added")
        s_st1 = sem("block1_statistics")
        s_gst1 = sem("block1_group_statistics")
        s_y1 = sem("gate_input")
        s_h1 = sem("gate_hidden")
        s_h1r = sem("gate_hidden_relu")
        s_gz = sem("gate_argument")
        s_gate = sem("gate_exponential")
        s_ab = sem("scale_ready")
        s_fin0 = sem("scaled_chunk0")
        s_fin1 = sem("scaled_chunk1")
        s_store = sem("stored")

        block = ctx.enter_context(nc.Block())

        def rows_of(fh, fw, g):
            return img[:, :, bass.ds(fh * RH + g * ROWS, ROWS), bass.ds(fw * RW, RW)]

        def regions(eng, n, body):
            with eng.Fori(0, 2) as fh:
                with eng.Fori(0, 2) as fw:
                    R = n * 4 + fh * 2 + fw
                    body(fh, fw, R, R * GROUPS)

        def pipeline(eng, step):
            step(0, 0, True, False, False)
            step(0, 1, True, True, False)
            with eng.Fori(1, PAIRS) as pair:
                step(pair, 0, True, True, True)
                step(pair, 1, True, True, True)
            step(PAIRS, 0, False, True, True)
            step(PAIRS, 1, False, False, True)

        def images(eng, body):
            if N > 1:
                with eng.Fori(0, N - 1) as n:
                    body(n, False)
            body(N - 1, True)

        STORES = 4
        SPX = H * W // (2 * STORES)

        @block.sync
        def _(sp):
            for dst, src in ((bp_s, bp_col), (bm_s, bm_col), (alpha_s, alpha), (beta_s, beta), (s0_s, first_centre),
                             (bvd0[:, :, :], bv_diag), (w1s[:, :, :], w1_t.rearrange("(k p) r -> p k r", p=P)),
                             (w2s[:, :], w2_t)):
                sp.dma_start(dst, src).then_inc(s_const, 16)
            sp.dma_start(raw[:, :, 0:C], wm_t.rearrange("(k p) d -> p k d", p=P)).then_inc(s_const, 16)

            def load_chunks(n, first):
                with sp.Fori(0, 2) as k:
                    with sp.Fori(0, UNITS) as u:
                        src = sp.snap(u * UNIT)
                        sp.wait_ge(s_chunk_used, first + k * UNITS + u)
                        sp.dma_start(chunk[:, :], xf[n, :, k, bass.ds(src, UNIT)]).then_inc(s_chunk, 16)

            def load_half(n, h, waits=()):
                with sp.Fori(0, STORES) as j:
                    o = sp.snap((h * STORES + j) * SPX)
                    for s, value in waits:
                        sp.wait_ge(s, value)
                    sp.dma_start(img[:, :, :, :].rearrange("p k h w -> p k (h w)")[:, :, bass.ds(o, SPX)],
                                 xf[n, :, :, bass.ds(o, SPX)]).then_inc(s_img, 16)

            load_chunks(0, 0)
            load_half(0, 0)
            sp.wait_ge(s_img, 16 * STORES)
            load_half(0, 1)

            def image(n, last):
                sp.wait_ge(s_raw_free, n + 1)
                sp.dma_start(raw[:, :, :], wp_t.rearrange("(k p) d -> p k d", p=P)).then_inc(s_raw, 16)
                if not last:
                    load_chunks(n + 1, (n + 1) * K * UNITS)
                with sp.Fori(0, 2) as h:
                    with sp.Fori(0, STORES) as j:
                        o = (h * STORES + j) * SPX
                        units = n * UNITS + (h * STORES + j + 1) * (UNITS // (2 * STORES))
                        sp.wait_ge(s_fin0, units)
                        sp.wait_ge(s_fin1, units)
                        sp.dma_start(of[n, :, :, bass.ds(o, SPX)],
                                     img[:, :, :, :].rearrange("p k h w -> p k (h w)")[:, :, bass.ds(o, SPX)]
                                     ).then_inc(s_store, 16)
                    if not last:
                        load_half(n + 1, h, ((s_store, (n * 2 + h + 1) * 16 * STORES),
                                             (s_img, (n * 2 + 2 + h) * 16 * STORES)))

            images(sp, image)
            sp.wait_ge(s_store, N * 2 * STORES * 16)

        @block.gpsimd
        def _(pool):
            pool.memset(ident[:, :], 0.0)
            pool.memset(identb[:, :], 0.0)
            pool.memset(gsum[:, :], 1.0 / 8)
            pool.memset(hsum[:, :, :], 1.0)
            pool.drain()
            pool.affine_select(out=ident[:, :], in_=ident[:, :], compare_op=ALU.not_equal, fill=1.0, base=0,
                               pattern=[[-1, P]], channel_multiplier=1)
            pool.affine_select(out=identb[:, :], in_=identb[:, :], compare_op=ALU.not_equal, fill=1.0, base=0,
                               pattern=[[-1, P]], channel_multiplier=1)
            gs = gsum[:, :].rearrange("p (j e) -> p j e", e=8)
            pool.affine_select(out=gs, in_=gs, compare_op=ALU.is_ge, fill=0.0, base=0,
                               pattern=[[-8, P // 8], [0, 8]], channel_multiplier=1)
            pool.affine_select(out=hsum[:, :, :], in_=hsum[:, :, :], compare_op=ALU.is_ge, fill=0.0, base=0,
                               pattern=[[-CH, HPM], [0, CH]], channel_multiplier=1)
            pool.drain()
            pool.affine_select(out=gs, in_=gs, compare_op=ALU.is_ge, fill=0.0, base=7,
                               pattern=[[8, P // 8], [0, 8]], channel_multiplier=-1)
            pool.affine_select(out=hsum[:, :, :], in_=hsum[:, :, :], compare_op=ALU.is_ge, fill=0.0, base=CH - 1,
                               pattern=[[CH, HPM], [0, CH]], channel_multiplier=-1)
            pool.drain().then_inc(s_ident, 1)
            for s in (s_xl, s_r1, s_v3, s_dl):
                pool.sem_inc(s, CREDIT)

            def region(fh, fw, R, G0):
                def low(g, q):
                    G = G0 + g
                    pool.wait_ge(s_xh, done(G))
                    pool.tensor_tensor(xl[:, q].rearrange("p k (a b) -> p k a b", b=RW), rows_of(fh, fw, g),
                                       xh[:, q].bitcast(F32).rearrange("p k (a b) -> p k a b", b=RW),
                                       ALU.subtract).then_inc(s_xl, 1)

                def step_a(pr, q, s1, s2, s3):
                    g = pr * 2 + q
                    G = G0 + g
                    if s1:
                        low(g, q)
                    if s3:
                        pool.wait_ge(s_v1, done(G - 2))
                        pool.tensor_tensor(vals, vals, vpart[0], ALU.subtract).then_inc(s_r1, 1)
                    if s3:
                        pool.wait_ge(s_v2, done(G - 2))
                        pool.tensor_tensor(vpart[2], vals, vpart[1], ALU.subtract).then_inc(s_v3, 1)

                pipeline(pool, step_a)

                def step_b(pr, q, s1, s2, s3):
                    g = pr * 2 + q
                    G = G0 + g
                    if s2:
                        pool.wait_ge(s_dh, done(G - 1))
                        pool.tensor_tensor(xl[:, 1 - q], sq[:, 1 - q], xh[:, 1 - q].bitcast(F32),
                                           ALU.subtract).then_inc(s_dl, 1)

                pipeline(pool, step_b)

            images(pool, lambda n, last: regions(pool, n, region))

        @block.scalar
        def _(act):
            for s in (s_xh, s_yh, s_sq, s_rn, s_ez, s_te, s_v1, s_v2, s_hs, s_dh):
                act.sem_inc(s, CREDIT)
            act.wait_ge(s_const, 16 * 9)
            act.wait_ge(s_zero, 1)
            nc.scalar.activation(lnn[:, 0:1], s0_s, ACT.Ln, scale=0.0, bias=lnbias)
            nc.scalar.activation(wmh[:, :, :], raw[:, :, 0:C], ACT.Copy).then_inc(s_wm, 1)

            def image(n, last):
                nc.scalar.preload_act_table_set("natural_log_exp_and_others")
                act.wait_ge(s_lnreq, 3 * n + 1)
                nc.scalar.activation(small[:, 12:14], small[:, 10:12], ACT.Ln)
                act.drain()
                nc.scalar.activation(small[:, 14:16], small[:, 12:14], ACT.Exp, scale=-0.5).then_inc(s_ln, 1)
                act.wait_ge(s_fold, n + 1)
                nc.scalar.activation(wph[:, :, :], raw[:, :, :], ACT.Copy).then_inc(s_wph, 1)
                act.wait_ge(s_lnreq, 3 * n + 2)
                nc.scalar.activation(gath[0], gath[1], ACT.Ln, scale=LN_SCALE)
                act.drain()
                nc.scalar.activation(gath[0], gath[0], ACT.Exp, scale=-0.5, bias=lnbias).then_inc(s_ln, 1)

                def region(fh, fw, R, G0):
                    act.wait_ge(s_o, before(G0))
                    act.wait_ge(s_img, (n * 2 + fh + 1) * 16 * STORES)

                    def high(g, q):
                        G = G0 + g
                        act.wait_ge(s_v, free(G))
                        act.wait_ge(s_xl, free(G))
                        nc.scalar.activation(xh[:, q].rearrange("p k (a b) -> p k a b", b=RW),
                                             rows_of(fh, fw, g), ACT.Copy).then_inc(s_xh, 1)

                    def step_a(pr, q, s1, s2, s3):
                        g = pr * 2 + q
                        G = G0 + g
                        if s1:
                            high(g, q)
                        if s3:
                            act.wait_ge(s_z, done(G - 2))
                            nc.scalar.activation(ez[:, :], zarg[:, q], ACT.Exp, scale=-1.0, bias=nbeta).then_inc(s_ez, 1)
                        if s2:
                            act.wait_ge(s_nc, done(G - 1))
                            nc.scalar.activation(lnn[:, :], rnorm[:, 1 - q], ACT.Ln, scale=LN_SCALE)
                            act.drain()
                            nc.scalar.activation(rnorm[:, 1 - q], lnn[:, :], ACT.Exp, scale=-0.5,
                                                 bias=lnbias).then_inc(s_rn, 1)
                        if s3:
                            act.wait_ge(s_t, done(G - 2))
                            nc.scalar.activation(hot_t[:, g - 2, :], bank[5][:, :].bitcast(BF16), ACT.Copy).then_inc(s_te, 1)
                            act.wait_ge(s_vs, done(G - 2))
                            act.wait_ge(s_agg, before(G - 2))
                            nc.scalar.activation(vpart[0], vals, ACT.Copy).then_inc(s_v1, 1)
                        if s1:
                            act.wait_ge(s_yp, done(G))
                            for m in range(M):
                                last_op = nc.scalar.activation(yh[:, m], y_ps[q][:, m], ACT.Identity, bias=bpf[:, m:m + 1])
                            last_op.then_inc(s_yh, 1)
                            for m in range(M):
                                last_op = nc.scalar.activation(sq[:, q, m], y_ps[q][:, m], ACT.Square, bias=bpf[:, m:m + 1])
                            last_op.then_inc(s_sq, 1)
                        if s3:
                            act.wait_ge(s_r1, done(G - 2))
                            nc.scalar.activation(vpart[1], vals, ACT.Copy).then_inc(s_v2, 1)

                    pipeline(act, step_a)

                    act.wait_ge(s_sum, R + 1)

                    def step_b(pr, q, s1, s2, s3):
                        g = pr * 2 + q
                        G = G0 + g
                        if s1:
                            act.wait_ge(s_g, free(G))
                            nc.scalar.activation(hot_s[:, q], hot_t[:, g, :], ACT.Copy).then_inc(s_hs, 1)
                        if s2:
                            act.wait_ge(s_dt, done(G - 1))
                            act.wait_ge(s_dl, free(G - 1))
                            act.wait_ge(s_o, free(G - 1))
                            nc.scalar.activation(xh[:, 1 - q], d_ps[1 - q], ACT.Copy)
                            nc.scalar.activation(sq[:, 1 - q], d_ps[1 - q], ACT.Copy).then_inc(s_dh, 1)

                    pipeline(act, step_b)

                regions(act, n, region)

                act.wait_ge(s_lnreq, 3 * n + 3)
                nc.scalar.activation(small[:, 32:34], small[:, 30:32], ACT.Ln)
                act.drain()
                nc.scalar.activation(small[:, 34:36], small[:, 32:34], ACT.Exp, scale=-0.5).then_inc(s_ln, 1)
                act.wait_ge(s_gz, n + 1)
                nc.scalar.activation(small[:, 44:46], n_ps[:, 0:2], ACT.Exp, scale=-1.0).then_inc(s_gate, 1)
                act.wait_ge(s_ab, n + 1)
                with act.Fori(0, UNITS) as u:
                    part = img[:, 0, bass.ds(u * CS, CS), :]
                    nc.scalar.activation(part, part, ACT.Identity, scale=small[:, 48:49],
                                         bias=small[:, 50:51]).then_inc(s_fin0, 1)

            images(act, image)

        @block.vector
        def _(dve):
            V = nc.vector
            for s in (s_yl, *s_hot, s_vs, s_nc, s_z, s_d, s_res):
                dve.sem_inc(s, CREDIT)
            V.memset(ch[:, :, :].bitcast(F32), 0.0)
            V.memset(cl[:, :, :].bitcast(F32), 0.0)
            V.memset(tab[:, :, :, :, :], 0.0)
            V.memset(zero[:, :], 0.0)
            V.memset(lnbias, LN2 * 10)
            dve.wait_ge(s_const, 16 * 9)
            V.tensor_scalar(nbeta, beta_s, -1.0, None, ALU.mult)
            V.tensor_scalar(keep_s, alpha_s, 0.0, None, ALU.not_equal)
            dve.drain().then_inc(s_zero, 1)
            V.tensor_tensor(keep_s, keep_s, s0_s, ALU.max)
            dve.wait_ge(s_wm, 1)
            V.tensor_tensor(wml[:, :, :], raw[:, :, 0:C], wmh[:, :, :].bitcast(F32), ALU.subtract)
            dve.drain()

            def chunk_moments(k, u):
                for j in range(2):
                    V.bn_stats(st[:, k, u * 2 + j, :], chunk[:, j * 512:(j + 1) * 512])

            def chunk_pool(k, u):
                V.tensor_reduce(pooled[:, k, u, :], chunk[:, :].rearrange("p (r b c) -> p b r c", r=CS, c=CS),
                                axis=AX.XY, op=ALU.add).then_inc(s_chunk_used, 1)

            with dve.Fori(0, K) as k:
                with dve.Fori(0, UNITS) as u:
                    dve.wait_ge(s_chunk, (k * UNITS + u + 1) * 16)
                    chunk_moments(k, u)
                    chunk_pool(k, u)

            def newton_rsqrt(r, v, t):
                V.tensor_tensor(t, r, r, ALU.mult)
                dve.drain()
                V.tensor_tensor(t, t, v, ALU.mult)
                dve.drain()
                V.tensor_scalar(t, t, -0.5, 1.5, ALU.mult, ALU.add)
                dve.drain()
                V.tensor_tensor(r, r, t, ALU.mult)
                dve.drain()

            def group_rstd(mean, var, rstd, log_count):
                V.tensor_copy(small[:, 16:20], n_ps[:, 0:4])
                dve.drain()
                sums = small[:, 16:20].rearrange("p (k e) -> p k e", e=2)
                V.tensor_copy(mean, sums[:, :, 0])
                V.tensor_tensor(small[:, 52:54], sums[:, :, 0], sums[:, :, 0], ALU.mult)
                dve.drain()
                V.tensor_tensor(var, sums[:, :, 1], small[:, 52:54], ALU.subtract)
                dve.drain()
                V.tensor_scalar(var, var, EPS, None, ALU.add)
                dve.drain().then_inc(s_lnreq, 1)
                dve.wait_ge(s_ln, log_count)
                newton_rsqrt(rstd, var, small[:, 52:54])

            def prepare(n):
                dve.drain().then_inc(s_raw_free, 1)
                for k in range(K):
                    V.bn_aggr(small[:, 2 * k:2 * k + 2], st[:, k].rearrange("p a b -> p (a b)"))
                dve.drain()
                mv_c = small[:, 0:4].rearrange("p (k e) -> p k e", e=2)
                sums = small[:, 4:8].rearrange("p (k e) -> p k e", e=2)
                V.tensor_copy(sums[:, :, 0], mv_c[:, :, 0])
                V.tensor_tensor(sums[:, :, 1], mv_c[:, :, 0], mv_c[:, :, 0], ALU.mult)
                dve.drain()
                V.tensor_tensor(sums[:, :, 1], sums[:, :, 1], mv_c[:, :, 1], ALU.add)
                dve.drain().then_inc(s_stat, 1)
                dve.wait_ge(s_gst, n + 1)
                group_rstd(small[:, 8:10], small[:, 10:12], small[:, 14:16], 3 * n + 1)
                dve.wait_ge(s_raw, 16 * (n + 1))
                for k in range(K):
                    V.tensor_scalar(raw[:, k], raw[:, k], small[:, 14 + k:15 + k], None, ALU.mult)
                    V.tensor_scalar((aggf, aggr)[k][:, :, :], hsum[:, :, :], 0.0, small[:, 8 + k:9 + k],
                                    ALU.mult, ALU.add)
                    for a in range(2):
                        V.tensor_copy(gath[1][:, k * 256 + a * 128:k * 256 + (a + 1) * 128].rearrange(
                            "p (b i j) -> p b i j", b=2, j=CS),
                            pooled[:, k, a * CS:(a + 1) * CS, :].rearrange("p i (b j) -> p b i j", j=CS))
                dve.drain().then_inc(s_fold, 1)
                dve.wait_ge(s_wph, n + 1)
                V.tensor_tensor(wpl[:, :, :], raw[:, :, :], wph[:, :, :].bitcast(F32), ALU.subtract).then_inc(s_wpl, 1)
                dve.wait_ge(s_cen, n + 1)
                V.tensor_tensor(bpf, bp_s, n_ps[:, 8:10], ALU.subtract)
                vb = bank[0][:, 0:C].rearrange("p (k j c) -> p k j c", k=KT, j=2)
                for j in range(2):
                    h = slice(64 * j, 64 * j + 64)
                    V.tensor_tensor(bvd[h], bvd0[h], vb[h, :, j, :], ALU.subtract)
                V.tensor_scalar(cvd[:, :, :, :].rearrange("p r k c -> p (r k c)"), bank[3][:, :],
                                1.0 / (CS * CS), None, ALU.mult)
                dve.drain()
                for m in range(M):
                    V.tensor_scalar(cen[:, m], bank[2][:, m * 256:(m + 1) * 256], 1.0 / (CS * CS), bpf[:, m:m + 1],
                                    ALU.mult, ALU.add)
                dve.drain()
                cenf = cen[:, :, :].rearrange("p m f -> p (m f)")
                V.tensor_tensor(gath[0], cenf, cenf, ALU.mult)
                dve.drain().then_inc(s_cenq, 1)
                dve.wait_ge(s_cenn, n + 1)
                V.tensor_scalar(gath[1], bank[0][:, :], NORM2_MIN, None, ALU.max)
                dve.drain().then_inc(s_lnreq, 1)
                dve.wait_ge(s_ln, 3 * n + 2)
                newton_rsqrt(gath[0], gath[1], newton)
                V.tensor_tensor(cenf, cenf, gath[0], ALU.mult)
                dve.drain()
                V.tensor_scalar(cenf, cenf, alpha_s, None, ALU.mult)
                dve.drain()

            def region_table(r, R):
                dve.wait_ge(s_sum, R + 1)
                halves = [slice(64 * j, 64 * j + 64) for j in range(2)]
                for j, h in enumerate(halves):
                    c0 = j * (CH + 1)
                    V.tensor_scalar(den[h], a_ps[h, :, c0 + CH:c0 + CH + 1], 1.0, None, ALU.add)
                    V.tensor_tensor(aggf[h], a_ps[h, :, c0:c0 + CH],
                                    cvd[h, bass.ds(r, 1)].rearrange("p o k c -> p (o k) c"), ALU.add)
                dve.drain()
                V.reciprocal(den[:, :, :], den[:, :, :])
                dve.drain()
                V.tensor_tensor(aggf[:, :, :], aggf[:, :, :], den[:, :, :].broadcast_to([P, KT, CH]), ALU.mult)
                dve.drain()
                V.tensor_tensor(aggf[:, :, :], aggf[:, :, :], bvd[:, :, :], ALU.add)
                dve.drain()
                V.tensor_scalar(aggf[:, :, :], aggf[:, :, :], keep_s, None, ALU.mult)
                for part in range(3):
                    dve.drain()
                    for j, h in enumerate(halves):
                        V.tensor_copy(tab[h, part, :, j, :], aggf[h])
                    if part < 2:
                        dve.drain()
                        for j, h in enumerate(halves):
                            V.tensor_tensor(aggf[h], aggf[h], tab[h, part, :, j, :], ALU.subtract)
                dve.drain().then_inc(s_tab, 1)

            def image(n, last):
                prepare(n)

                def region(fh, fw, R, G0):
                    r = fh * 2 + fw
                    c0 = (n + 1) * K * UNITS + r * PAIRS
                    blocks = []
                    for h in range(HPM):
                        p = slice(CH * h, CH * h + CH)
                        src = cen[p, :, :].rearrange("p m (a b) -> p m a b", b=UNITS)[
                            :, :, bass.ds(fh * CS, CS), bass.ds(fw * CS, CS)]
                        dst = [t[p, :, h * CENTRES:(h + 1) * CENTRES] for t in (ch, cl)]
                        blocks.append((src, *dst))
                    for src, hi, lo in blocks:
                        V.tensor_copy(hi.rearrange("p m (a b) -> p m a b", b=CS), src)
                    dve.drain()
                    for src, hi, lo in blocks:
                        V.tensor_tensor(lo.rearrange("p m (a b) -> p m a b", b=CS), src,
                                        hi.bitcast(F32).rearrange("p m (a b) -> p m a b", b=CS), ALU.subtract)
                    dve.drain().then_inc(s_c, 1)

                    def step_a(pr, q, s1, s2, s3):
                        g = pr * 2 + q
                        G = G0 + g
                        if s2:
                            dve.wait_ge(s_n2, done(G - 1))
                            V.tensor_scalar(rnorm[:, 1 - q], n_ps[:, 16 * (1 - q):16 * (2 - q)], NORM2_MIN, None,
                                            ALU.max).then_inc(s_nc, 1)
                        if s3:
                            dve.wait_ge(s_ez, done(G - 2))
                            V.tensor_scalar(ez[:, :], ez[:, :], 1.0, None, ALU.add)
                            dve.drain()
                            dve.wait_ge(s_v3, before(G - 2))
                            sig = mv[:, bass.ds((g - 2) * TILES, TILES), :]
                            V.reciprocal(sig.rearrange("p t h -> p (t h)"), ez[:, :])
                            dve.drain()
                            dve.wait_ge(s_v, done(G - 2))
                            V.tensor_tensor(vals[:, :, :, 0:CH].rearrange("p t h c -> p (t h) c"),
                                            v_ps.rearrange("p t h c -> p (t h) c"),
                                            sig.rearrange("p t (h o) -> p (t h) o", o=1).broadcast_to(
                                                [P, TILES * HEADS, CH]), ALU.mult)
                            V.tensor_copy(vals[:, :, :, CH:CH + 1].rearrange("p t h o -> p (t h) o"),
                                          sig.rearrange("p t (h o) -> p (t h) o", o=1)).then_inc(s_vs, 1)
                        if s2:
                            for t in range(TILES):
                                dve.wait_ge(s_sim[t], done(G - 1))
                                sims = s_ps[t][:, :].rearrange("p (h s) -> p h s", h=HEADS)
                                V.tensor_reduce(rank[:, 1 - q, t], sims, axis=AX.X, op=ALU.max)
                                dve.drain()
                                dve.wait_ge(s_agg, free(G - 1))
                                V.tensor_tensor(hot[:, 1 - q, t].rearrange("p (h s) -> p h s", h=HEADS), sims,
                                                rank[:, 1 - q, t].rearrange("p (h o) -> p h o", o=1).broadcast_to(
                                                    [P, HEADS, CENTRES]), ALU.is_equal).then_inc(s_hot[t], 1)
                        if s1:
                            dve.wait_ge(s_yh, done(G))
                            dve.wait_ge(s_sq, done(G))
                            for m in range(M):
                                op = V.scalar_tensor_tensor(yl[:, m], y_ps[q][:, m], bpf[:, m:m + 1],
                                                            yh[:, m].bitcast(F32), ALU.add, ALU.subtract)
                            op.then_inc(s_yl, 1)
                        if s2:
                            dve.wait_ge(s_rn, done(G - 1))
                            V.tensor_tensor(zarg[:, 1 - q], rank[:, 1 - q].rearrange("p t h -> p (t h)"),
                                            rnorm[:, 1 - q], ALU.mult).then_inc(s_z, 1)
                        if s1 and not last:
                            if q == 0:
                                dve.wait_ge(s_chunk, (c0 + pr + 1) * 16)
                                chunk_moments(fh, fw * PAIRS + pr)
                            else:
                                chunk_pool(fh, fw * PAIRS + pr)

                    pipeline(dve, step_a)
                    region_table(r, R)

                    def step_b(pr, q, s1, s2, s3):
                        g = pr * 2 + q
                        G = G0 + g
                        if s1:
                            dve.wait_ge(s_g, done(G))
                            dve.wait_ge(s_dt, free(G))
                            V.tensor_tensor(gath[q].rearrange("p (a c) -> p a c", c=CH),
                                            g_ps[q][:, :].rearrange("p (a c) -> p a c", c=CH),
                                            mv[:, bass.ds(g * TILES, TILES), :].rearrange("p t (h o) -> p (t h) o", o=1)
                                            .broadcast_to([P, TILES * HEADS, CH]), ALU.mult).then_inc(s_d, 1)
                        if s3:
                            dve.wait_ge(s_o, done(G - 2))
                            rows = rows_of(fh, fw, g - 2)
                            V.tensor_tensor(rows, rows, o_ps[q].rearrange("p m (a b) -> p m a b", b=RW),
                                            ALU.add).then_inc(s_res, 1)
                            dve.drain()
                            for m in range(M):
                                V.bn_stats(st1[:, m, g - 2, :], rows[:, m])

                    pipeline(dve, step_b)
                    dve.drain()
                    for m in range(M):
                        V.bn_aggr(pair[:, m], st1[:, m].rearrange("p a b -> p (a b)"))
                    dve.drain()
                    V.tensor_copy(agg1[:, bass.ds(r, 1)].rearrange("p o m e -> p (o m) e"), pair[:, :, :])
                    dve.drain()

                regions(dve, n, region)

                V.tensor_tensor(e2[:, :, :], agg1[:, :, :, 0], agg1[:, :, :, 0], ALU.mult)
                dve.drain()
                V.tensor_tensor(e2[:, :, :], e2[:, :, :], agg1[:, :, :, 1], ALU.add)
                V.tensor_reduce(small[:, 22:24], agg1[:, :, :, 0].rearrange("p r m -> p m r"), axis=AX.X, op=ALU.add)
                V.tensor_reduce(small[:, 24:26], diagonal, axis=AX.X, op=ALU.add)
                dve.drain()
                V.tensor_reduce(small[:, 56:58], e2[:, :, :].rearrange("p r m -> p m r"), axis=AX.X, op=ALU.add)
                V.tensor_scalar(small[:, 22:24], small[:, 22:24], 0.25, None, ALU.mult)
                dve.drain()
                V.tensor_tensor(small[:, 54:56], small[:, 22:24], small[:, 22:24], ALU.mult)
                V.tensor_scalar(small[:, 56:58], small[:, 56:58], 0.25, None, ALU.mult)
                sums1 = small[:, 58:62].rearrange("p (k e) -> p k e", e=2)
                V.tensor_tensor(sums1[:, :, 0], small[:, 22:24], bm_s, ALU.add)
                dve.drain()
                V.tensor_tensor(small[:, 56:58], small[:, 56:58], small[:, 54:56], ALU.subtract)
                V.tensor_tensor(small[:, 62:64], sums1[:, :, 0], sums1[:, :, 0], ALU.mult)
                dve.drain()
                V.tensor_tensor(sums1[:, :, 1], small[:, 56:58], small[:, 62:64], ALU.add)
                V.tensor_scalar(small[:, 24:26], small[:, 24:26], 1.0 / W, None, ALU.mult)
                dve.drain().then_inc(s_st1, 1)
                dve.wait_ge(s_gst1, n + 1)
                V.tensor_tensor(small[:, 24:26], small[:, 24:26], bm_s, ALU.add)
                group_rstd(small[:, 26:28], small[:, 30:32], small[:, 34:36], 3 * n + 3)
                V.tensor_tensor(small[:, 24:26], small[:, 24:26], small[:, 26:28], ALU.subtract)
                dve.drain()
                V.tensor_tensor(small[:, 36:38], small[:, 24:26], small[:, 34:36], ALU.mult)
                dve.drain().then_inc(s_y1, 1)
                dve.wait_ge(s_h1, n + 1)
                V.tensor_scalar(small[0:HIDDEN, 40:41], n_ps[0:HIDDEN, 8:9], 0.0, None, ALU.max)
                dve.drain().then_inc(s_h1r, 1)
                dve.wait_ge(s_gate, n + 1)
                V.tensor_scalar(small[:, 44:46], small[:, 44:46], 1.0, None, ALU.add)
                dve.drain()
                V.reciprocal(small[:, 42:44], small[:, 44:46])
                dve.drain()
                V.tensor_tensor(small[:, 46:48], small[:, 42:44], small[:, 34:36], ALU.mult)
                dve.drain()
                V.tensor_scalar(small[:, 48:50], small[:, 46:48], 1.0, None, ALU.add)
                V.tensor_tensor(small[:, 52:54], small[:, 46:48], small[:, 26:28], ALU.mult)
                dve.drain()
                V.tensor_tensor(small[:, 50:52], small[:, 48:50], bm_s, ALU.mult)
                dve.drain()
                V.tensor_tensor(small[:, 50:52], small[:, 50:52], small[:, 52:54], ALU.subtract)
                dve.drain().then_inc(s_ab, 1)
                with dve.Fori(0, UNITS) as u:
                    part = img[:, 1, bass.ds(u * CS, CS), :]
                    V.tensor_scalar(part, part, small[:, 49:50], small[:, 51:52], ALU.mult, ALU.add).then_inc(s_fin1, 1)

            images(dve, image)

        @block.tensor
        def _(pe):
            mm = nc.tensor.matmul
            for s in (s_yp, *s_sim, s_v, s_n2, s_t, s_agg, s_g, s_dt, s_o):
                pe.sem_inc(s, CREDIT)
            pe.wait_ge(s_ident, 1)
            pe.wait_ge(s_zero, 1)

            def three(out, terms):
                passes = [(a, b) for (ah, al), (bh, bl) in terms for a, b in ((ah, bh), (ah, bl), (al, bh))]
                for i, (a, b) in enumerate(passes):
                    op = mm(out, a, b, start=i == 0, stop=i == len(passes) - 1)
                return op

            def image(n, last):
                pe.wait_ge(s_stat, n + 1)
                mm(n_ps[:, 0:4], gsum[:, :], small[:, 4:8], start=True, stop=True).then_inc(s_gst, 1)
                pe.wait_ge(s_fold, n + 1)
                for m in range(M):
                    for k in range(K):
                        mm(n_ps[:, 8 + m:9 + m], raw[:, k, m * P:(m + 1) * P], small[:, 8 + k:9 + k],
                           start=k == 0, stop=k == K - 1)
                for k in range(K):
                    mm(bank[0][:, 0:C], (aggf, aggr)[k][:, :, :].rearrange("p a b -> p (a b)"), raw[:, k, C:2 * C],
                       start=k == 0, stop=k == K - 1)
                for m in range(M):
                    for k in range(K):
                        mm(bank[2][:, m * 256:(m + 1) * 256], raw[:, k, m * P:(m + 1) * P],
                           pooled[:, k].rearrange("p a b -> p (a b)"), start=k == 0, stop=k == K - 1)
                for r in range(4):
                    for j in range(2):
                        for k in range(K):
                            op = mm(bank[3][64 * j:64 * j + 64, r * P:(r + 1) * P],
                                    gath[1][:, k * 256 + r * CENTRES:k * 256 + (r + 1) * CENTRES],
                                    raw[:, k, C:2 * C].rearrange("p (t j c) -> p t j c", j=2, c=CH)[:, :, j, :],
                                    start=k == 0, stop=k == K - 1)
                op.then_inc(s_cen, 1)
                pe.wait_ge(s_cenq, n + 1)
                mm(bank[0][:, :], hsum[:, :, :].rearrange("p a b -> p (a b)"), gath[0], start=True,
                   stop=True).then_inc(s_cenn, 1)

                def region(fh, fw, R, G0):
                    pe.wait_ge(s_wpl, n + 1)
                    pe.wait_ge(s_c, R + 1)
                    pe.wait_ge(s_res, before(G0))
                    mm(a_ps, zero[:, 0:P], zero[:, :].rearrange("p (k c) -> p k c", k=KT), start=True, stop=False,
                       skip_group_check=True)

                    def step_a(pr, q, s1, s2, s3):
                        g = pr * 2 + q
                        G = G0 + g
                        if s2:
                            pe.wait_ge(s_yh, done(G - 1))
                            pe.wait_ge(s_yl, done(G - 1))
                            for t in range(TILES):
                                px = slice(t * P, (t + 1) * P)
                                pe.wait_ge(s_hot[t], before(G - 1))
                                for m in range(M):
                                    op = three(s_ps[t][:, m * 256:(m + 1) * 256],
                                               [((yh[:, m, px], yl[:, m, px]), (ch[:, m], cl[:, m]))])
                                op.then_inc(s_sim[t], 1)
                        if s1:
                            pe.wait_ge(s_xh, done(G))
                            pe.wait_ge(s_xl, done(G))
                            pe.wait_ge(s_yl, free(G))
                            for m in range(M):
                                d = slice(m * P, (m + 1) * P)
                                op = three(y_ps[q][:, m], [((wph[:, k, d], wpl[:, k, d]), (xh[:, q, k], xl[:, q, k]))
                                                           for k in range(K)])
                            op.then_inc(s_yp, 1)
                        if s3:
                            pe.wait_ge(s_te, before(G - 2))
                            for t in range(TILES):
                                pe.wait_ge(s_hot[t], done(G - 2))
                                for kt in range(KT):
                                    op = nc.tensor.transpose(t_ps[:, kt, t * P:(t + 1) * P],
                                                             hot[:, q, t, kt * P:(kt + 1) * P], identb[:, :])
                            op.then_inc(s_t, 1)
                        if s2:
                            pe.wait_ge(s_vs, before(G - 1))
                            for t in range(TILES):
                                px = slice(t * P, (t + 1) * P)
                                op = three(v_ps[:, t].rearrange("p h c -> p (h c)"),
                                           [((xh[:, 1 - q, k, px], xl[:, 1 - q, k, px]),
                                             (wph[:, k, C:2 * C], wpl[:, k, C:2 * C])) for k in range(K)])
                            op.then_inc(s_v, 1)
                        if s3:
                            pe.wait_ge(s_v3, done(G - 2))
                            for t in range(TILES):
                                for kt in range(KT):
                                    for part in range(3):
                                        op = mm(a_ps[:, kt, :], hot[:, q, t, kt * P:(kt + 1) * P],
                                                vpart[part][:, t, 2 * kt:2 * kt + 2, :].rearrange("p h c -> p (h c)"),
                                                start=False, stop=False, skip_group_check=True)
                            op.then_inc(s_agg, 1)
                        if s1:
                            pe.wait_ge(s_sq, done(G))
                            pe.wait_ge(s_nc, before(G))
                            for t in range(TILES):
                                for m in range(M):
                                    c = 16 * q + HEADS * t + HPM * m
                                    op = mm(n_ps[:, c:c + HPM], sq[:, q, m, t * P:(t + 1) * P], hsum[:, :, 0],
                                            start=True, stop=True)
                            op.then_inc(s_n2, 1)

                    pipeline(pe, step_a)
                    mm(a_ps, zero[:, 0:P], zero[:, :].rearrange("p (k c) -> p k c", k=KT), start=False, stop=True,
                       skip_group_check=True).then_inc(s_sum, 1)
                    pe.wait_ge(s_tab, R + 1)
                    pe.wait_ge(s_te, before(G0 + GROUPS))

                    def step_b(pr, q, s1, s2, s3):
                        g = pr * 2 + q
                        G = G0 + g
                        if s1:
                            pe.wait_ge(s_hs, done(G))
                            pe.wait_ge(s_d, free(G))
                            for t in range(TILES):
                                for kt in range(KT):
                                    c = t * 256 + kt * 64
                                    for part in range(3):
                                        op = mm(g_ps[q][:, c:c + 64], hot_s[:, q, kt * PX + t * P:kt * PX + (t + 1) * P],
                                                tab[:, part, kt].rearrange("p j c -> p (j c)"),
                                                start=part == 0, stop=part == 2)
                            op.then_inc(s_g, 1)
                        if s2:
                            pe.wait_ge(s_d, done(G - 1))
                            pe.wait_ge(s_dh, free(G - 1))
                            for m in range(M):
                                for t in range(TILES):
                                    c = t * 256 + m * P
                                    op = nc.tensor.transpose(d_ps[1 - q][:, m, t * P:(t + 1) * P],
                                                             gath[1 - q][:, c:c + P], ident[:, :])
                            op.then_inc(s_dt, 1)
                        if s3:
                            pe.wait_ge(s_dh, done(G - 2))
                            pe.wait_ge(s_dl, done(G - 2))
                            pe.wait_ge(s_res, free(G - 2))
                            for m in range(M):
                                d = slice(m * P, (m + 1) * P)
                                op = three(o_ps[q][:, m], [((wmh[:, k, d], wml[:, k, d]), (xh[:, q, k], xl[:, q, k]))
                                                           for k in range(M)])
                            op.then_inc(s_o, 1)

                    pipeline(pe, step_b)

                regions(pe, n, region)

                pe.wait_ge(s_st1, n + 1)
                mm(n_ps[:, 0:4], gsum[:, :], small[:, 58:62], start=True, stop=True).then_inc(s_gst1, 1)
                pe.wait_ge(s_y1, n + 1)
                for k in range(K):
                    op = mm(n_ps[0:HIDDEN, 8:9], w1s[:, k, :], small[:, 36 + k:37 + k], start=k == 0, stop=k == K - 1)
                op.then_inc(s_h1, 1)
                pe.wait_ge(s_h1r, n + 1)
                for m in range(M):
                    op = mm(n_ps[:, m:m + 1], w2s[:, m * P:(m + 1) * P], small[0:HIDDEN, 40:41], start=True, stop=True)
                op.then_inc(s_gz, 1)

            images(pe, image)


def kernel(**inputs):
    import numpy as _np
    import concourse.bacc as _bacc
    from concourse import mybir as _mybir
    from concourse.bass_utils import run_bass_kernel_spmd as _run

    a = {k: _np.asarray(v) for k, v in inputs.items()}
    C = a["x"].shape[1]
    wp = a["L0_conv_Wp"].reshape(HEADS, 2, CH, C)
    bp = a["L0_conv_bp"].reshape(HEADS, 2, CH)
    bv = bp[:, 1, :].reshape(HEADS // 2, 2, CH).transpose(1, 0, 2)
    first = _np.zeros((P, 1), _np.float32)
    first[::CENTRES] = 1.0
    arrays = {
        "x": a["x"],
        "wp_t": wp.transpose(3, 1, 0, 2).reshape(C, 2 * C),
        "bp_col": bp[:, 0, :].reshape(2, P).T,
        "bv_diag": _np.repeat(bv, CENTRES, axis=0),
        "wm_t": a["L0_conv_Wm"].T,
        "bm_col": a["L0_conv_bm"].reshape(2, P).T,
        "alpha": _np.repeat(a["L0_conv_alpha"].reshape(1, 1), P, axis=0),
        "beta": _np.repeat(a["L0_conv_beta"].reshape(1, 1), P, axis=0),
        "w1_t": a["L1_conv_w1"].T,
        "w2_t": a["L1_conv_w2"].T,
        "first_centre": first,
    }
    nc = _bacc.Bacc("TRN2", target_bir_lowering=False, num_devices=1)
    args = []
    for name in arrays:
        arrays[name] = _np.ascontiguousarray(arrays[name])
        args.append(nc.dram_tensor(name, arrays[name].shape, _mybir.dt.from_np(arrays[name].dtype),
                                   kind="ExternalInput").ap())
    args.append(nc.dram_tensor("out", a["x"].shape, _mybir.dt.from_np(a["x"].dtype), kind="ExternalOutput").ap())
    cluster_block(nc, *args)
    return _run(nc, [arrays], core_ids=[0]).results[0]["out"]
```

```python
from contextlib import ExitStack

import concourse.bass as bass
from concourse import mybir

F32 = mybir.dt.float32
F32R = mybir.dt.float32r
BF16 = mybir.dt.bfloat16
U8 = mybir.dt.uint8
ALU = mybir.AluOpType
ACT = mybir.ActivationFunctionType
AX = mybir.AxisListType

P = 128
HEADS = 8
CH = 32
CENTRES = 64
CS = 8
EPS = 1e-5
NORM2_MIN = 1e-24
LN_SCALE = 2.0 ** 20
LN2 = 0.6931471805599453

CREDIT = 2


def done(group):
    return group + 1 + CREDIT


def free(group):
    return group + 1


def before(group):
    return group + CREDIT


def cluster_block(nc, x, wp_t, bp_col, bv_diag, wm_t, bm_col, alpha, beta, w1_t, w2_t, first_centre, out):
    N, C, H, W = x.shape
    K = C // P
    RH, RW = H // 2, W // 2
    ROWS = 4
    PX = ROWS * RW
    TILES = PX // P
    GROUPS = RH // ROWS
    PAIRS = GROUPS // 2
    KT = HEADS // 2
    HS = HEADS * CENTRES
    M = HEADS * CH // P
    HPM = HEADS // M
    UNIT = CS * W
    UNITS = H // CS
    AGG = 2 * (CH + 1)
    HIDDEN = w1_t.shape[1]

    xf = x.rearrange("n (k p) h w -> n p k (h w)", p=P)
    of = out.rearrange("n (k p) h w -> n p k (h w)", p=P)

    ctx = ExitStack()
    with ctx:
        def sb(name, shape, dt=F32):
            return ctx.enter_context(nc.sbuf_tensor(name, shape, dt))

        def sem(name):
            return ctx.enter_context(nc.semaphore(name))

        img = sb("img", [P, K, H, W])
        hot_t = sb("hot_t", [P, GROUPS, KT * PX], U8)
        mv = sb("mv", [P, GROUPS * TILES, HEADS])
        xh = sb("xh", [P, 2, K, PX], F32R)
        xl = sb("xl", [P, 2, K, PX], F32R)
        yh = sb("yh", [P, M, PX], F32R)
        yl = sb("yl", [P, M, PX], F32R)
        sq = sb("sq", [P, 2, M, PX])
        hot = sb("hot", [P, 2, TILES, HS], BF16)
        work = sb("work", [P, 3696], BF16)
        VSIZE = TILES * HEADS * (CH + 1)
        vals = [work[:, 2 * VSIZE * b:2 * VSIZE * (b + 1)].bitcast(F32).rearrange(
            "p (t h c) -> p t h c", t=TILES, h=HEADS) for b in range(2)]
        vpart = [work[:, VSIZE * (4 + i):VSIZE * (5 + i)].rearrange("p (t h c) -> p t h c", t=TILES, h=HEADS)
                 for i in range(3)]
        hot_s = work[:, 0:2 * KT * PX].rearrange("p (b f) -> p b f", b=2)
        gath = [hot[:, b, :, :].rearrange("p t f -> p (t f)").bitcast(F32) for b in range(2)]
        raw_wm = gath[0].rearrange("p (k d) -> p k d", k=M)
        newton = work[:, 0:1024].bitcast(F32)
        rank = sb("rank", [P, 2, TILES, HEADS])
        rnorm = sb("rnorm", [P, 2, TILES * HEADS])
        lnn = sb("lnn", [P, TILES * HEADS])
        zero = sb("zero", [P, KT * AGG], BF16)
        zarg = sb("zarg", [P, 2, TILES * HEADS])
        ez = sb("ez", [P, TILES * HEADS])
        wph = sb("wph", [P, K, 2 * C], F32R)
        wpl = sb("wpl", [P, K, 2 * C], F32R)
        wmh = sb("wmh", [P, M, C], F32R)
        wml = sb("wml", [P, M, C], F32R)
        ch = sb("ch", [P, M, HPM * CENTRES], F32R)
        cl = sb("cl", [P, M, HPM * CENTRES], F32R)
        tab = sb("tab", [P, 3, KT, 2, CH], BF16)
        aggf = sb("aggf", [P, KT, CH])
        aggr = sb("aggr", [P, KT, CH])
        den = sb("den", [P, KT, 1])
        chunk = sb("chunk", [P, UNIT])
        pooled = sb("pooled", [P, K, UNITS, UNITS])
        usum = sb("usum", [P, K, UNITS])
        st1 = sb("st1", [P, M, GROUPS, 6])
        agg1 = sb("agg1", [P, 5, M, 2])
        cen = sb("cen", [P, (4 * M + 1) * CENTRES])
        cvd = sb("cvd", [P, 4, KT, CH])
        bvd0 = sb("bvd0", [P, KT, CH])
        bvd = sb("bvd", [P, KT, CH])
        ident = sb("ident", [P, P])
        identb = sb("identb", [P, P], BF16)
        gsum = sb("gsum", [P, P])
        small = sb("small", [P, 64])
        hsum = sb("hsum", [P, HPM, CH])
        pair = sb("pair", [P, M, 2])
        e2 = sb("e2", [P, 4, M])
        w1s = sb("w1s", [P, K, HIDDEN])
        w2s = sb("w2s", [HIDDEN, C])
        cols = sb("cols", [P, 16])
        bp_s, bm_s = cols[:, 0:2], cols[:, 2:4]
        alpha_s, beta_s, s0_s, keep_s = cols[:, 4:5], cols[:, 5:6], cols[:, 6:7], cols[:, 7:8]
        bpf = cols[:, 8:10]
        nbeta = cols[:, 10:11]
        lnbias = cols[:, 11:12]

        ysq = sq[:, 0]
        raw = sq[:, :, :, :].rearrange("p a m f -> p (a m f)").rearrange("p (k d) -> p k d", k=K)

        bank = [ctx.enter_context(nc.psum_tensor(f"bank{i}", [P, 512], F32)) for i in range(8)]
        y_ps = bank[0][:, :].rearrange("p (m f) -> p m f", m=M)
        s_ps = [bank[2], bank[3]]
        v_ps = [bank[i][:, :].rearrange("p (t h c) -> p t h c", t=TILES, h=HEADS) for i in (4, 1)]
        t_ps = bank[5][:, :].bitcast(BF16).rearrange("p (k f) -> p k f", k=KT)
        a_ps = bank[6][:, 0:KT * AGG].rearrange("p (k c) -> p k c", k=KT)
        n_ps = bank[7]
        g_ps = [bank[0], bank[1]]
        d_ps = [bank[4][:, :].rearrange("p (m f) -> p m f", m=M), bank[5][:, :].rearrange("p (m f) -> p m f", m=M)]
        o_ps = [bank[2][:, :].rearrange("p (m f) -> p m f", m=M), bank[3][:, :].rearrange("p (m f) -> p m f", m=M)]

        junk = hot_t[:, 0:4, :].rearrange("p g f -> p (g f)").bitcast(F32)
        usq = cols[:, 12:13]
        diagonal = img[:, :, :, :].rearrange("p k h w -> p k (h w)")[:, :, 0:H * W:W + 1]

        s_const = sem("const_loaded")
        s_zero = sem("cleared")
        s_ident = sem("identity_ready")
        s_wm = sem("mix_weights_split")
        s_img = sem("image_units_in")
        s_load = [sem("unit_loaded0"), sem("unit_loaded1")]
        s_chunk = sem("chunk_loaded")
        s_sum0 = sem("first_image_squared")
        s_pooled = sem("chunk_pooled")
        s_chunk_used = sem("chunk_used")
        s_raw = sem("weights_loaded")
        s_raw_free = sem("weights_place_free")
        s_stat = sem("statistics_ready")
        s_gst = sem("group_statistics_summed")
        s_fold = sem("weights_folded")
        s_wph = sem("folded_high")
        s_wpl = sem("folded_low")
        s_cen = sem("centres_projected")
        s_cenq = sem("centres_squared")
        s_cenn = sem("centres_norms")
        s_cv = sem("centre_values")
        s_cvd = sem("centre_values_taken")
        s_ln = sem("logs")
        s_lnreq = sem("log_asked")
        s_c = sem("region_centres_ready")
        s_xh = sem("x_high")
        s_xl = sem("x_low")
        s_yp = sem("projected")
        s_yh = sem("y_high")
        s_sq = sem("squared")
        s_yl = sem("y_low")
        s_sim = [sem("similar0"), sem("similar1")]
        s_hot = [sem("one_hot0"), sem("one_hot1")]
        s_v = sem("values")
        s_vs = sem("values_scaled")
        s_n2 = sem("norms")
        s_nc = sem("norms_guarded")
        s_rn = sem("norms_inverted")
        s_z = sem("argument")
        s_ez = sem("exponential")
        s_t = sem("transposed")
        s_te = sem("transposed_kept")
        s_v1 = sem("values_part1")
        s_r1 = sem("values_rest1")
        s_v2 = sem("values_part2")
        s_v3 = sem("values_part3")
        s_agg = sem("aggregated")
        s_sum = sem("region_summed")
        s_tab = sem("region_table_ready")
        s_hs = sem("hot_widened")
        s_g = sem("gathered")
        s_d = sem("weighted")
        s_dt = sem("weighted_transposed")
        s_dh = sem("weighted_high")
        s_dl = sem("weighted_low")
        s_o = sem("mixed")
        s_res = sem("added")
        s_st1 = sem("block1_statistics")
        s_gst1 = sem("block1_group_statistics")
        s_y1 = sem("gate_input")
        s_h1 = sem("gate_hidden")
        s_h1r = sem("gate_hidden_relu")
        s_gz = sem("gate_argument")
        s_gate = sem("gate_exponential")
        s_ab = sem("scale_ready")
        s_fin = [sem("scaled_by_act"), sem("scaled_by_dve")]
        s_store = [sem("unit_stored0"), sem("unit_stored1")]

        block = ctx.enter_context(nc.Block())

        def rows_of(fh, fw, g):
            return img[:, :, bass.ds(fh * RH + g * ROWS, ROWS), bass.ds(fw * RW, RW)]

        def regions(eng, n, body):
            with eng.Fori(0, 2) as fh:
                with eng.Fori(0, 2) as fw:
                    R = n * 4 + fh * 2 + fw
                    body(fh, fw, R, R * GROUPS)

        STAGES = 4

        def first_step(pair, q, step):
            return isinstance(pair, int) and 2 * pair + q == step

        def pipeline(eng, step):
            def one(pair, q):
                i = 2 * pair + q
                step(pair, q, [0 <= i - k < GROUPS for k in range(STAGES)])
            for i in range(STAGES):
                one(i // 2, i % 2)
            with eng.Fori(STAGES // 2, PAIRS) as pair:
                step(pair, 0, [True] * STAGES)
                step(pair, 1, [True] * STAGES)
            for i in range(GROUPS, GROUPS + STAGES - 1):
                one(i // 2, i % 2)

        def images(eng, body):
            if N > 1:
                with eng.Fori(0, N - 1) as n:
                    body(n, False)
            body(N - 1, True)

        ACT_ROWS = 6

        @block.sync
        def _(sp):
            for dst, src in ((bp_s, bp_col), (bm_s, bm_col), (alpha_s, alpha), (beta_s, beta), (s0_s, first_centre),
                             (bvd0[:, :, :], bv_diag), (w1s[:, :, :], w1_t.rearrange("(k p) r -> p k r", p=P)),
                             (w2s[:, :], w2_t)):
                sp.dma_start(dst, src).then_inc(s_const, 16)
            sp.dma_start(raw_wm, wm_t.rearrange("(k p) d -> p k d", p=P)).then_inc(s_const, 16)

            def load_chunks(n, first):
                with sp.Fori(0, 2) as k:
                    with sp.Fori(0, UNITS) as u:
                        src = sp.snap(u * UNIT)
                        sp.wait_ge(s_chunk_used, first + k * UNITS + u)
                        sp.dma_start(chunk[:, :], xf[n, :, k, bass.ds(src, UNIT)]).then_inc(s_chunk, 16)

            units_of = img[:, :, :, :].rearrange("p k h w -> p k (h w)")

            def load_unit(n, u, q):
                o = sp.snap(u * UNIT)
                sp.dma_start(units_of[:, :, bass.ds(o, UNIT)], xf[n, :, :, bass.ds(o, UNIT)]).then_inc(s_load[q], 16)

            def loaded(count, q):
                sp.wait_ge(s_load[q], 16 * count)
                sp.sem_inc(s_img, 1)

            load_unit(0, 0, 0)
            sp.dma_start(raw[:, :, :], wp_t.rearrange("(k p) d -> p k d", p=P)).then_inc(s_raw, 16)
            load_unit(0, 1, 1)
            with sp.Fori(1, UNITS // 2) as v:
                for q in range(2):
                    loaded(v, q)
                    load_unit(0, v * 2 + q, q)
            loaded(UNITS // 2, 0)
            loaded(UNITS // 2, 1)

            def image(n, last):
                if not last:
                    load_chunks(n + 1, n * K * UNITS)
                half = UNITS // 2

                def store_unit(u, q):
                    o = sp.snap(u * UNIT)
                    for s in s_fin:
                        sp.wait_ge(s, n * UNITS + u + 1)
                    sp.dma_start(of[n, :, :, bass.ds(o, UNIT)], units_of[:, :, bass.ds(o, UNIT)]).then_inc(s_store[q], 16)

                if last:
                    with sp.Fori(0, half) as v:
                        for q in range(2):
                            store_unit(v * 2 + q, q)
                    return
                store_unit(0, 0)
                sp.wait_ge(s_raw_free, n + 1)
                sp.dma_start(raw[:, :, :], wp_t.rearrange("(k p) d -> p k d", p=P)).then_inc(s_raw, 16)
                store_unit(1, 1)
                sp.wait_ge(s_store[0], (n * half + 1) * 16)
                load_unit(n + 1, 0, 0)
                with sp.Fori(1, half) as v:
                    store_unit(v * 2, 0)
                    sp.wait_ge(s_store[1], (n * half + v) * 16)
                    load_unit(n + 1, v * 2 - 1, 1)
                    loaded((n + 1) * half + v, 0)
                    store_unit(v * 2 + 1, 1)
                    sp.wait_ge(s_store[0], (n * half + v + 1) * 16)
                    load_unit(n + 1, v * 2, 0)
                    loaded((n + 1) * half + v, 1)
                sp.wait_ge(s_store[1], (n + 1) * half * 16)
                load_unit(n + 1, UNITS - 1, 1)
                loaded((n + 2) * half, 0)
                loaded((n + 2) * half, 1)

            images(sp, image)
            for s in s_store:
                sp.wait_ge(s, N * UNITS // 2 * 16)

        @block.gpsimd
        def _(pool):
            pool.memset(ident[:, :], 0.0)
            pool.memset(identb[:, :], 0.0)
            pool.memset(gsum[:, :], 1.0 / 8)
            pool.memset(hsum[:, :, :], 1.0)
            pool.drain()
            pool.affine_select(out=ident[:, :], in_=ident[:, :], compare_op=ALU.not_equal, fill=1.0, base=0,
                               pattern=[[-1, P]], channel_multiplier=1)
            pool.affine_select(out=identb[:, :], in_=identb[:, :], compare_op=ALU.not_equal, fill=1.0, base=0,
                               pattern=[[-1, P]], channel_multiplier=1)
            gs = gsum[:, :].rearrange("p (j e) -> p j e", e=8)
            pool.affine_select(out=gs, in_=gs, compare_op=ALU.is_ge, fill=0.0, base=0,
                               pattern=[[-8, P // 8], [0, 8]], channel_multiplier=1)
            pool.affine_select(out=hsum[:, :, :], in_=hsum[:, :, :], compare_op=ALU.is_ge, fill=0.0, base=0,
                               pattern=[[-CH, HPM], [0, CH]], channel_multiplier=1)
            pool.drain()
            pool.affine_select(out=gs, in_=gs, compare_op=ALU.is_ge, fill=0.0, base=7,
                               pattern=[[8, P // 8], [0, 8]], channel_multiplier=-1)
            pool.affine_select(out=hsum[:, :, :], in_=hsum[:, :, :], compare_op=ALU.is_ge, fill=0.0, base=CH - 1,
                               pattern=[[CH, HPM], [0, CH]], channel_multiplier=-1)
            pool.drain().then_inc(s_ident, 1)
            for s in (s_xl, s_r1, s_v3, s_dl):
                pool.sem_inc(s, CREDIT)

            def region(fh, fw, R, G0):
                def step_a(pr, q, on):
                    g = pr * 2 + q
                    G = G0 + g
                    if on[3]:
                        pool.wait_ge(s_v1, done(G - 3))
                        pool.tensor_tensor(vals[1 - q], vals[1 - q], vpart[0], ALU.subtract).then_inc(s_r1, 1)
                        pool.wait_ge(s_v2, done(G - 3))
                        pool.tensor_tensor(vpart[2], vals[1 - q], vpart[1], ALU.subtract).then_inc(s_v3, 1)
                    if on[0]:
                        pool.wait_ge(s_xh, done(G))
                        pool.tensor_tensor(xl[:, q].rearrange("p k (a b) -> p k a b", b=RW), rows_of(fh, fw, g),
                                           xh[:, q].bitcast(F32).rearrange("p k (a b) -> p k a b", b=RW),
                                           ALU.subtract).then_inc(s_xl, 1)

                pipeline(pool, step_a)

                def step_b(pr, q, on):
                    G = G0 + pr * 2 + q
                    if on[2]:
                        pool.wait_ge(s_dh, done(G - 2))
                        pool.tensor_tensor(xl[:, q], sq[:, q], xh[:, q].bitcast(F32), ALU.subtract).then_inc(s_dl, 1)

                pipeline(pool, step_b)

            images(pool, lambda n, last: regions(pool, n, region))

        @block.scalar
        def _(act):
            for s in (s_xh, s_yh, s_sq, s_rn, s_ez, s_te, s_v1, s_v2, s_hs, s_dh):
                act.sem_inc(s, CREDIT)
            act.wait_ge(s_const, 16 * 9)
            act.wait_ge(s_zero, 1)
            nc.scalar.activation(lnn[:, 0:1], s0_s, ACT.Ln, scale=0.0, bias=lnbias)
            nc.scalar.activation(wmh[:, :, :], raw_wm, ACT.Copy).then_inc(s_wm, 1)

            with act.Fori(0, UNITS) as u:
                for k in range(K):
                    act.wait_ge(s_img, u + 1)
                    nc.scalar.activation(junk, img[:, k, bass.ds(u * CS, CS), :].rearrange("p a b -> p (a b)"),
                                         ACT.Square, accum_out=usq)
                    act.drain()
                    nc.scalar.activation(usum[:, k, bass.ds(u, 1)], usq, ACT.Copy)
                    act.drain()
            act.drain().then_inc(s_sum0, 1)

            def image(n, last):
                nc.scalar.preload_act_table_set("natural_log_exp_and_others")
                act.wait_ge(s_lnreq, 3 * n + 1)
                nc.scalar.activation(small[:, 12:14], small[:, 10:12], ACT.Ln)
                act.drain()
                nc.scalar.activation(small[:, 14:16], small[:, 12:14], ACT.Exp, scale=-0.5).then_inc(s_ln, 1)
                act.wait_ge(s_fold, n + 1)
                nc.scalar.activation(wph[:, :, :], raw[:, :, :], ACT.Copy).then_inc(s_wph, 1)
                act.wait_ge(s_lnreq, 3 * n + 2)
                nc.scalar.activation(gath[0], gath[1], ACT.Ln, scale=LN_SCALE)
                act.drain()
                nc.scalar.activation(gath[0], gath[0], ACT.Exp, scale=-0.5, bias=lnbias).then_inc(s_ln, 1)

                def region(fh, fw, R, G0):
                    def step_a(pr, q, on):
                        g = pr * 2 + q
                        G = G0 + g
                        if on[3]:
                            act.wait_ge(s_vs, done(G - 3))
                            act.wait_ge(s_agg, before(G - 3))
                            nc.scalar.activation(vpart[0], vals[1 - q], ACT.Copy).then_inc(s_v1, 1)
                        if on[2]:
                            act.wait_ge(s_nc, done(G - 2))
                            nc.scalar.activation(lnn[:, :], rnorm[:, q], ACT.Ln, scale=LN_SCALE)
                            act.drain()
                            nc.scalar.activation(rnorm[:, q], lnn[:, :], ACT.Exp, scale=-0.5,
                                                 bias=lnbias).then_inc(s_rn, 1)
                        if on[0]:
                            act.wait_ge(s_img, n * UNITS + fh * PAIRS + pr + 1)
                            act.wait_ge(s_v, free(G))
                            act.wait_ge(s_xl, free(G))
                            if first_step(pr, q, 0) or first_step(pr, q, 1):
                                act.wait_ge(s_o, free(G))
                            nc.scalar.activation(xh[:, q].rearrange("p k (a b) -> p k a b", b=RW),
                                                 rows_of(fh, fw, g), ACT.Copy).then_inc(s_xh, 1)
                        if on[3]:
                            act.wait_ge(s_r1, done(G - 3))
                            nc.scalar.activation(vpart[1], vals[1 - q], ACT.Copy).then_inc(s_v2, 1)
                        if on[2]:
                            act.wait_ge(s_z, done(G - 2))
                            nc.scalar.activation(ez[:, :], zarg[:, q], ACT.Exp, scale=-1.0, bias=nbeta).then_inc(s_ez, 1)
                        if on[1]:
                            act.wait_ge(s_yp, done(G - 1))
                            for m in range(M):
                                op = nc.scalar.activation(yh[:, m], y_ps[:, m], ACT.Identity, bias=bpf[:, m:m + 1])
                            op.then_inc(s_yh, 1)
                            act.wait_ge(s_n2, before(G - 1))
                            for m in range(M):
                                op = nc.scalar.activation(ysq[:, m], y_ps[:, m], ACT.Square, bias=bpf[:, m:m + 1])
                            op.then_inc(s_sq, 1)
                        if on[3]:
                            act.wait_ge(s_t, done(G - 3))
                            nc.scalar.activation(hot_t[:, g - 3, :], bank[5][:, :].bitcast(BF16), ACT.Copy
                                                 ).then_inc(s_te, 1)
                        if on[0] and q == 1 and not last:
                            act.wait_ge(s_pooled, n * K * UNITS + (fh * 2 + fw) * PAIRS + pr + 1)
                            nc.scalar.activation(chunk[:, :], chunk[:, :], ACT.Square, accum_out=usq)
                            act.drain()
                            nc.scalar.activation(usum[:, fh, bass.ds(fw * PAIRS + pr, 1)], usq, ACT.Copy
                                                 ).then_inc(s_chunk_used, 1)

                    pipeline(act, step_a)

                    act.wait_ge(s_sum, R + 1)

                    def step_b(pr, q, on):
                        g = pr * 2 + q
                        G = G0 + g
                        if on[0]:
                            act.wait_ge(s_g, free(G))
                            nc.scalar.activation(hot_s[:, q], hot_t[:, g, :], ACT.Copy).then_inc(s_hs, 1)
                        if on[2]:
                            act.wait_ge(s_dt, done(G - 2))
                            act.wait_ge(s_dl, free(G - 2))
                            act.wait_ge(s_o, free(G - 2))
                            nc.scalar.activation(xh[:, q], d_ps[q], ACT.Copy)
                            nc.scalar.activation(sq[:, q], d_ps[q], ACT.Copy).then_inc(s_dh, 1)

                    pipeline(act, step_b)

                regions(act, n, region)

                act.wait_ge(s_lnreq, 3 * n + 3)
                nc.scalar.activation(small[:, 32:34], small[:, 30:32], ACT.Ln)
                act.drain()
                nc.scalar.activation(small[:, 34:36], small[:, 32:34], ACT.Exp, scale=-0.5).then_inc(s_ln, 1)
                act.wait_ge(s_gz, n + 1)
                nc.scalar.activation(small[:, 44:46], n_ps[:, 0:2], ACT.Exp, scale=-1.0).then_inc(s_gate, 1)
                act.wait_ge(s_ab, n + 1)
                with act.Fori(0, UNITS) as u:
                    part = img[:, 0, bass.ds(u * CS, ACT_ROWS), :]
                    nc.scalar.activation(part, part, ACT.Identity, scale=small[:, 48:49],
                                         bias=small[:, 50:51]).then_inc(s_fin[0], 1)

            images(act, image)

        @block.vector
        def _(dve):
            V = nc.vector
            for s in (*s_hot, s_vs, s_nc, s_z, s_d, s_res, s_yl):
                dve.sem_inc(s, CREDIT)
            V.memset(ch[:, :, :].bitcast(F32), 0.0)
            V.memset(cl[:, :, :].bitcast(F32), 0.0)
            V.memset(tab[:, :, :, :, :], 0.0)
            V.memset(zero[:, :], 0.0)
            V.memset(cen[:, :], 0.0)
            V.memset(st1[:, :, :, :], 1.0)
            V.memset(lnbias, LN2 * 10)
            dve.wait_ge(s_const, 16 * 9)
            V.tensor_scalar(nbeta, beta_s, -1.0, None, ALU.mult)
            V.tensor_scalar(keep_s, alpha_s, 0.0, None, ALU.not_equal)
            dve.drain().then_inc(s_zero, 1)
            V.tensor_tensor(keep_s, keep_s, s0_s, ALU.max)
            dve.wait_ge(s_wm, 1)
            V.tensor_tensor(wml[:, :, :], raw_wm, wmh[:, :, :].bitcast(F32), ALU.subtract)
            dve.drain()

            def pool_chunk(src, k, u):
                return V.tensor_reduce(pooled[:, k, u, :], src.rearrange("p (r b c) -> p b r c", r=CS, c=CS),
                                       axis=AX.XY, op=ALU.add)

            with dve.Fori(0, UNITS) as u:
                dve.wait_ge(s_img, u + 1)
                for k in range(K):
                    pool_chunk(img[:, k, bass.ds(u * CS, CS), :].rearrange("p a b -> p (a b)"), k, u)
            dve.drain()
            dve.wait_ge(s_sum0, 1)

            def newton_rsqrt(r, v, t):
                V.tensor_tensor(t, r, r, ALU.mult)
                dve.drain()
                V.tensor_tensor(t, t, v, ALU.mult)
                dve.drain()
                V.tensor_scalar(t, t, -0.5, 1.5, ALU.mult, ALU.add)
                dve.drain()
                V.tensor_tensor(r, r, t, ALU.mult)
                dve.drain()

            def group_rstd(mean, var, rstd, log_count):
                V.tensor_copy(small[:, 16:20], n_ps[:, 0:4])
                dve.drain()
                sums = small[:, 16:20].rearrange("p (k e) -> p k e", e=2)
                V.tensor_copy(mean, sums[:, :, 0])
                V.tensor_tensor(small[:, 52:54], sums[:, :, 0], sums[:, :, 0], ALU.mult)
                dve.drain()
                V.tensor_tensor(var, sums[:, :, 1], small[:, 52:54], ALU.subtract)
                dve.drain()
                V.tensor_scalar(var, var, EPS, None, ALU.add)
                dve.drain().then_inc(s_lnreq, 1)
                dve.wait_ge(s_ln, log_count)
                newton_rsqrt(rstd, var, small[:, 52:54])

            def prepare(n):
                sums = small[:, 4:8].rearrange("p (k e) -> p k e", e=2)
                dve.wait_ge(s_chunk_used, n * K * UNITS)
                V.tensor_reduce(sums[:, :, 0:1], pooled[:, :, :, :], axis=AX.XY, op=ALU.add)
                V.tensor_reduce(sums[:, :, 1:2], usum[:, :, :], axis=AX.X, op=ALU.add)
                dve.drain()
                V.tensor_scalar(small[:, 4:8], small[:, 4:8], 1.0 / (H * W), None, ALU.mult)
                dve.drain().then_inc(s_stat, 1)
                dve.wait_ge(s_gst, n + 1)
                group_rstd(small[:, 8:10], small[:, 10:12], small[:, 14:16], 3 * n + 1)
                dve.wait_ge(s_raw, 16 * (n + 1))
                for k in range(K):
                    V.tensor_scalar(raw[:, k], raw[:, k], small[:, 14 + k:15 + k], None, ALU.mult)
                    V.tensor_scalar((aggf, aggr)[k][:, :, :], hsum[:, :, :], 0.0, small[:, 8 + k:9 + k],
                                    ALU.mult, ALU.add)
                    for a in range(2):
                        V.tensor_copy(gath[1][:, k * 256 + a * 128:k * 256 + (a + 1) * 128].rearrange(
                            "p (b i j) -> p b i j", b=2, j=CS),
                            pooled[:, k, a * CS:(a + 1) * CS, :].rearrange("p i (b j) -> p b i j", j=CS))
                dve.drain().then_inc(s_fold, 1)
                dve.wait_ge(s_wph, n + 1)
                V.tensor_tensor(wpl[:, :, :], raw[:, :, :], wph[:, :, :].bitcast(F32), ALU.subtract).then_inc(s_wpl, 1)
                dve.wait_ge(s_cen, n + 1)
                V.tensor_tensor(bpf, bp_s, n_ps[:, 8:10], ALU.subtract)
                vb = bank[0][:, 0:C].rearrange("p (k j c) -> p k j c", k=KT, j=2)
                for j in range(2):
                    h = slice(64 * j, 64 * j + 64)
                    V.tensor_tensor(bvd[h], bvd0[h], vb[h, :, j, :], ALU.subtract)
                dve.drain()
                V.tensor_scalar(bvd[:, :, :], bvd[:, :, :], keep_s, None, ALU.mult)
                V.tensor_scalar(cvd[:, :, :, :].rearrange("p r k c -> p (r k c)"), bank[3][:, :],
                                1.0 / (CS * CS), None, ALU.mult)
                dve.drain()
                cenf = cen[:, 0:4 * M * CENTRES]
                for m in range(M):
                    V.tensor_scalar(cenf[:, m * 256:(m + 1) * 256], bank[2][:, m * 256:(m + 1) * 256], 1.0 / (CS * CS), bpf[:, m:m + 1],
                                    ALU.mult, ALU.add)
                dve.drain()
                V.tensor_tensor(gath[0], cenf, cenf, ALU.mult)
                dve.drain().then_inc(s_cenq, 1)
                dve.wait_ge(s_cenn, n + 1)
                V.tensor_scalar(gath[1], bank[0][:, :], NORM2_MIN, None, ALU.max)
                dve.drain().then_inc(s_lnreq, 1)
                dve.wait_ge(s_ln, 3 * n + 2)
                newton_rsqrt(gath[0], gath[1], newton)
                V.tensor_tensor(cenf, cenf, gath[0], ALU.mult)
                dve.drain()
                V.tensor_scalar(cenf, cenf, alpha_s, None, ALU.mult)
                dve.drain()
                region_centres(0)

            def region_centres(r):
                blocks = []
                for m in range(M):
                    for h in range(HPM):
                        p = slice(CH * h, CH * h + CH)
                        src = cen[p, bass.ds(r * CENTRES + m * 4 * CENTRES, CENTRES)]
                        blocks.append((src, *[t[p, m, h * CENTRES:(h + 1) * CENTRES] for t in (ch, cl)]))
                for src, hi, lo in blocks:
                    V.tensor_copy(hi, src)
                dve.drain()
                for src, hi, lo in blocks:
                    V.tensor_tensor(lo, src, hi.bitcast(F32), ALU.subtract)
                dve.drain().then_inc(s_c, 1)

            def region_statistics(r):
                for m in range(M):
                    V.bn_aggr(pair[:, m], st1[:, m].rearrange("p a b -> p (a b)"))
                dve.drain()
                V.tensor_copy(agg1[:, bass.ds(r + 1, 1)].rearrange("p o m e -> p (o m) e"), pair[:, :, :])
                dve.drain()

            def region_table(r, R):
                dve.wait_ge(s_sum, R + 1)
                halves = [slice(64 * j, 64 * j + 64) for j in range(2)]
                for j, h in enumerate(halves):
                    c0 = j * (CH + 1)
                    V.tensor_scalar(den[h], a_ps[h, :, c0 + CH:c0 + CH + 1], 1.0, None, ALU.add)
                    V.tensor_tensor(aggf[h], a_ps[h, :, c0:c0 + CH],
                                    cvd[h, bass.ds(r, 1)].rearrange("p o k c -> p (o k) c"), ALU.add)
                dve.drain()
                V.reciprocal(den[:, :, :], den[:, :, :])
                dve.drain()
                V.scalar_tensor_tensor(aggf[:, :, :], aggf[:, :, :], keep_s, den[:, :, :].broadcast_to([P, KT, CH]),
                                       ALU.mult, ALU.mult)
                dve.drain()
                V.tensor_tensor(aggf[:, :, :], aggf[:, :, :], bvd[:, :, :], ALU.add)
                for part in range(3):
                    dve.drain()
                    for j, h in enumerate(halves):
                        op = V.tensor_copy(tab[h, part, :, j, :], aggf[h])
                    op.then_inc(s_tab, 1)
                    if part < 2:
                        dve.drain()
                        for j, h in enumerate(halves):
                            V.tensor_tensor(aggf[h], aggf[h], tab[h, part, :, j, :], ALU.subtract)

            def image(n, last):
                prepare(n)

                def region(fh, fw, R, G0):
                    r = fh * 2 + fw
                    def step_a(pr, q, on):
                        g = pr * 2 + q
                        G = G0 + g
                        if on[2]:
                            dve.wait_ge(s_n2, done(G - 2))
                            V.tensor_scalar(rnorm[:, q], n_ps[:, 16 * q:16 * (q + 1)], NORM2_MIN, None,
                                            ALU.max).then_inc(s_nc, 1)
                            sims = [s_ps[t][:, :].rearrange("p (h s) -> p h s", h=HEADS) for t in range(TILES)]
                            for t in range(TILES):
                                dve.wait_ge(s_sim[t], done(G - 2))
                                V.tensor_reduce(rank[:, q, t], sims[t], axis=AX.X, op=ALU.max)
                            dve.drain()
                            dve.wait_ge(s_rn, done(G - 2))
                            V.tensor_tensor(zarg[:, q], rank[:, q].rearrange("p t h -> p (t h)"), rnorm[:, q],
                                            ALU.mult).then_inc(s_z, 1)
                            dve.wait_ge(s_agg, free(G - 2))
                            for t in range(TILES):
                                V.tensor_tensor(hot[:, q, t].rearrange("p (h s) -> p h s", h=HEADS), sims[t],
                                                rank[:, q, t].rearrange("p (h o) -> p h o", o=1).broadcast_to(
                                                    [P, HEADS, CENTRES]), ALU.is_equal).then_inc(s_hot[t], 1)
                            dve.wait_ge(s_ez, done(G - 2))
                            V.tensor_scalar(ez[:, :], ez[:, :], 1.0, None, ALU.add)
                            dve.drain()
                            sig = mv[:, bass.ds((g - 2) * TILES, TILES), :]
                            V.reciprocal(sig.rearrange("p t h -> p (t h)"), ez[:, :])
                        if on[1]:
                            dve.wait_ge(s_sq, done(G - 1))
                            for m in range(M):
                                op = V.scalar_tensor_tensor(yl[:, m], y_ps[:, m], bpf[:, m:m + 1],
                                                            yh[:, m].bitcast(F32), ALU.add, ALU.subtract)
                            op.then_inc(s_yl, 1)
                        if on[2]:
                            dve.drain()
                            dve.wait_ge(s_v, done(G - 2))
                            dve.wait_ge(s_v3, free(G - 2))
                            V.tensor_tensor(vals[q][:, :, :, 0:CH].rearrange("p t h c -> p (t h) c"),
                                            v_ps[q].rearrange("p t h c -> p (t h) c"),
                                            sig.rearrange("p t (h o) -> p (t h) o", o=1).broadcast_to(
                                                [P, TILES * HEADS, CH]), ALU.mult)
                            V.tensor_copy(vals[q][:, :, :, CH:CH + 1].rearrange("p t h o -> p (t h) o"),
                                          sig.rearrange("p t (h o) -> p (t h) o", o=1)).then_inc(s_vs, 1)
                        if on[0] and q == 0 and not last:
                            dve.wait_ge(s_chunk, (n * K * UNITS + r * PAIRS + pr + 1) * 16)
                            pool_chunk(chunk[:, :], fh, fw * PAIRS + pr).then_inc(s_pooled, 1)

                    pipeline(dve, step_a)
                    region_statistics(r - 1)
                    region_table(r, R)

                    def step_b(pr, q, on):
                        g = pr * 2 + q
                        G = G0 + g
                        if on[1]:
                            dve.wait_ge(s_g, done(G - 1))
                            dve.wait_ge(s_dt, free(G - 1))
                            V.tensor_tensor(gath[1 - q].rearrange("p (a c) -> p a c", c=CH),
                                            g_ps[1 - q][:, :].rearrange("p (a c) -> p a c", c=CH),
                                            mv[:, bass.ds((g - 1) * TILES, TILES), :].rearrange(
                                                "p t (h o) -> p (t h) o", o=1).broadcast_to([P, TILES * HEADS, CH]),
                                            ALU.mult).then_inc(s_d, 1)
                        if first_step(pr, q, 2):
                            region_centres(r + 1)
                        if on[3]:
                            dve.wait_ge(s_o, done(G - 3))
                            rows = rows_of(fh, fw, g - 3)
                            V.tensor_tensor(rows, rows, o_ps[1 - q].rearrange("p m (a b) -> p m a b", b=RW),
                                            ALU.add).then_inc(s_res, 1)
                            dve.drain()
                            for m in range(M):
                                V.bn_stats(st1[:, m, g - 3, :], rows[:, m])

                    pipeline(dve, step_b)
                    dve.drain()

                regions(dve, n, region)
                if not last:
                    dve.sem_inc(s_raw_free, 1)
                region_statistics(3)

                V.tensor_tensor(e2[:, :, :], agg1[:, 1:5, :, 0], agg1[:, 1:5, :, 0], ALU.mult)
                dve.drain()
                V.tensor_tensor(e2[:, :, :], e2[:, :, :], agg1[:, 1:5, :, 1], ALU.add)
                V.tensor_reduce(small[:, 22:24], agg1[:, 1:5, :, 0].rearrange("p r m -> p m r"), axis=AX.X, op=ALU.add)
                V.tensor_reduce(small[:, 24:26], diagonal, axis=AX.X, op=ALU.add)
                dve.drain()
                V.tensor_reduce(small[:, 56:58], e2[:, :, :].rearrange("p r m -> p m r"), axis=AX.X, op=ALU.add)
                V.tensor_scalar(small[:, 22:24], small[:, 22:24], 0.25, None, ALU.mult)
                dve.drain()
                V.tensor_tensor(small[:, 54:56], small[:, 22:24], small[:, 22:24], ALU.mult)
                V.tensor_scalar(small[:, 56:58], small[:, 56:58], 0.25, None, ALU.mult)
                sums1 = small[:, 58:62].rearrange("p (k e) -> p k e", e=2)
                V.tensor_tensor(sums1[:, :, 0], small[:, 22:24], bm_s, ALU.add)
                dve.drain()
                V.tensor_tensor(small[:, 56:58], small[:, 56:58], small[:, 54:56], ALU.subtract)
                V.tensor_tensor(small[:, 62:64], sums1[:, :, 0], sums1[:, :, 0], ALU.mult)
                dve.drain()
                V.tensor_tensor(sums1[:, :, 1], small[:, 56:58], small[:, 62:64], ALU.add)
                V.tensor_scalar(small[:, 24:26], small[:, 24:26], 1.0 / W, None, ALU.mult)
                dve.drain().then_inc(s_st1, 1)
                dve.wait_ge(s_gst1, n + 1)
                V.tensor_tensor(small[:, 24:26], small[:, 24:26], bm_s, ALU.add)
                group_rstd(small[:, 26:28], small[:, 30:32], small[:, 34:36], 3 * n + 3)
                V.tensor_tensor(small[:, 24:26], small[:, 24:26], small[:, 26:28], ALU.subtract)
                dve.drain()
                V.tensor_tensor(small[:, 36:38], small[:, 24:26], small[:, 34:36], ALU.mult)
                dve.drain().then_inc(s_y1, 1)
                dve.wait_ge(s_h1, n + 1)
                V.tensor_scalar(small[0:HIDDEN, 40:41], n_ps[0:HIDDEN, 8:9], 0.0, None, ALU.max)
                dve.drain().then_inc(s_h1r, 1)
                dve.wait_ge(s_gate, n + 1)
                V.tensor_scalar(small[:, 44:46], small[:, 44:46], 1.0, None, ALU.add)
                dve.drain()
                V.reciprocal(small[:, 42:44], small[:, 44:46])
                dve.drain()
                V.tensor_tensor(small[:, 46:48], small[:, 42:44], small[:, 34:36], ALU.mult)
                dve.drain()
                V.tensor_scalar(small[:, 48:50], small[:, 46:48], 1.0, None, ALU.add)
                V.tensor_tensor(small[:, 52:54], small[:, 46:48], small[:, 26:28], ALU.mult)
                dve.drain()
                V.tensor_tensor(small[:, 50:52], small[:, 48:50], bm_s, ALU.mult)
                dve.drain()
                V.tensor_tensor(small[:, 50:52], small[:, 50:52], small[:, 52:54], ALU.subtract)
                dve.drain().then_inc(s_ab, 1)
                with dve.Fori(0, UNITS) as u:
                    part = img[:, 0, bass.ds(u * CS + ACT_ROWS, CS - ACT_ROWS), :]
                    V.tensor_scalar(part, part, small[:, 48:49], small[:, 50:51], ALU.mult, ALU.add)
                    part = img[:, 1, bass.ds(u * CS, CS), :]
                    V.tensor_scalar(part, part, small[:, 49:50], small[:, 51:52], ALU.mult, ALU.add).then_inc(s_fin[1], 1)

            images(dve, image)

        @block.tensor
        def _(pe):
            mm = nc.tensor.matmul
            for s in (s_yp, *s_sim, s_v, s_n2, s_t, s_agg, s_g, s_dt, s_o):
                pe.sem_inc(s, CREDIT)
            pe.wait_ge(s_ident, 1)
            pe.wait_ge(s_zero, 1)

            def three(out, terms):
                passes = [(a, b) for (ah, al), (bh, bl) in terms for a, b in ((ah, bh), (ah, bl), (al, bh))]
                for i, (a, b) in enumerate(passes):
                    op = mm(out, a, b, start=i == 0, stop=i == len(passes) - 1)
                return op

            def image(n, last):
                pe.wait_ge(s_stat, n + 1)
                mm(n_ps[:, 0:4], gsum[:, :], small[:, 4:8], start=True, stop=True).then_inc(s_gst, 1)
                pe.wait_ge(s_fold, n + 1)
                for m in range(M):
                    for k in range(K):
                        mm(n_ps[:, 8 + m:9 + m], raw[:, k, m * P:(m + 1) * P], small[:, 8 + k:9 + k],
                           start=k == 0, stop=k == K - 1)
                for k in range(K):
                    mm(bank[0][:, 0:C], (aggf, aggr)[k][:, :, :].rearrange("p a b -> p (a b)"), raw[:, k, C:2 * C],
                       start=k == 0, stop=k == K - 1)
                for m in range(M):
                    for k in range(K):
                        mm(bank[2][:, m * 256:(m + 1) * 256], raw[:, k, m * P:(m + 1) * P],
                           gath[1][:, k * 256:(k + 1) * 256], start=k == 0, stop=k == K - 1)
                for r in range(4):
                    for j in range(2):
                        for k in range(K):
                            op = mm(bank[3][64 * j:64 * j + 64, r * P:(r + 1) * P],
                                    gath[1][:, k * 256 + r * CENTRES:k * 256 + (r + 1) * CENTRES],
                                    raw[:, k, C:2 * C].rearrange("p (t j c) -> p t j c", j=2, c=CH)[:, :, j, :],
                                    start=k == 0, stop=k == K - 1)
                op.then_inc(s_cen, 1)
                pe.wait_ge(s_cenq, n + 1)
                mm(bank[0][:, :], hsum[:, :, :].rearrange("p a b -> p (a b)"), gath[0], start=True,
                   stop=True).then_inc(s_cenn, 1)

                def region(fh, fw, R, G0):
                    pe.wait_ge(s_wpl, n + 1)
                    pe.wait_ge(s_c, R + n + 1)
                    pe.wait_ge(s_d, before(G0))
                    pe.wait_ge(s_dh, before(G0))
                    mm(a_ps, zero[:, 0:P], zero[:, :].rearrange("p (k c) -> p k c", k=KT), start=True, stop=False,
                       skip_group_check=True)

                    def step_a(pr, q, on):
                        G = G0 + pr * 2 + q
                        if on[2]:
                            if first_step(pr, q, 2):
                                pe.wait_ge(s_res, before(G0))
                            pe.wait_ge(s_yh, done(G - 2))
                            pe.wait_ge(s_yl, done(G - 2))
                            for t in range(TILES):
                                px = slice(t * P, (t + 1) * P)
                                pe.wait_ge(s_hot[t], before(G - 2))
                                for m in range(M):
                                    op = three(s_ps[t][:, m * 256:(m + 1) * 256],
                                               [((yh[:, m, px], yl[:, m, px]), (ch[:, m], cl[:, m]))])
                                op.then_inc(s_sim[t], 1)
                        if on[1]:
                            pe.wait_ge(s_xh, done(G - 1))
                            pe.wait_ge(s_xl, done(G - 1))
                            pe.wait_ge(s_sq, before(G - 1))
                            pe.wait_ge(s_yl, before(G - 1))
                            for m in range(M):
                                d = slice(m * P, (m + 1) * P)
                                op = three(y_ps[:, m],
                                           [((wph[:, k, d], wpl[:, k, d]), (xh[:, 1 - q, k], xl[:, 1 - q, k]))
                                            for k in range(K)])
                            op.then_inc(s_yp, 1)
                        if on[3]:
                            pe.wait_ge(s_te, before(G - 3))
                            for t in range(TILES):
                                pe.wait_ge(s_hot[t], done(G - 3))
                                for kt in range(KT):
                                    op = nc.tensor.transpose(t_ps[:, kt, t * P:(t + 1) * P],
                                                             hot[:, 1 - q, t, kt * P:(kt + 1) * P], identb[:, :])
                            op.then_inc(s_t, 1)
                        if on[1]:
                            pe.wait_ge(s_vs, free(G - 1))
                            for t in range(TILES):
                                px = slice(t * P, (t + 1) * P)
                                op = three(v_ps[1 - q][:, t].rearrange("p h c -> p (h c)"),
                                           [((xh[:, 1 - q, k, px], xl[:, 1 - q, k, px]),
                                             (wph[:, k, C:2 * C], wpl[:, k, C:2 * C])) for k in range(K)])
                            op.then_inc(s_v, 1)
                        if on[3]:
                            pe.wait_ge(s_v3, done(G - 3))
                            for t in range(TILES):
                                for kt in range(KT):
                                    for part in range(3):
                                        op = mm(a_ps[:, kt, :], hot[:, 1 - q, t, kt * P:(kt + 1) * P],
                                                vpart[part][:, t, 2 * kt:2 * kt + 2, :].rearrange("p h c -> p (h c)"),
                                                start=False, stop=False, skip_group_check=True)
                            op.then_inc(s_agg, 1)
                        if on[1]:
                            pe.wait_ge(s_sq, done(G - 1))
                            pe.wait_ge(s_nc, before(G - 1))
                            for t in range(TILES):
                                for m in range(M):
                                    c = 16 * (1 - q) + HEADS * t + HPM * m
                                    op = mm(n_ps[:, c:c + HPM], ysq[:, m, t * P:(t + 1) * P], hsum[:, :, 0],
                                            start=True, stop=True)
                            op.then_inc(s_n2, 1)

                    pipeline(pe, step_a)
                    mm(a_ps, zero[:, 0:P], zero[:, :].rearrange("p (k c) -> p k c", k=KT), start=False, stop=True,
                       skip_group_check=True).then_inc(s_sum, 1)
                    pe.wait_ge(s_te, before(G0 + GROUPS))

                    def step_b(pr, q, on):
                        g = pr * 2 + q
                        G = G0 + g
                        if on[1]:
                            pe.wait_ge(s_hs, done(G - 1))
                            pe.wait_ge(s_d, free(G - 1))
                            if first_step(pr, q, 1):
                                pe.wait_ge(s_tab, 3 * (R + 1))
                            for t in range(TILES):
                                for kt in range(KT):
                                    c = t * 256 + kt * 64
                                    for part in range(3):
                                        op = mm(g_ps[1 - q][:, c:c + 64],
                                                hot_s[:, 1 - q, kt * PX + t * P:kt * PX + (t + 1) * P],
                                                tab[:, part, kt].rearrange("p j c -> p (j c)"),
                                                start=part == 0, stop=part == 2)
                            op.then_inc(s_g, 1)
                        if on[2]:
                            pe.wait_ge(s_d, done(G - 2))
                            pe.wait_ge(s_dh, free(G - 2))
                            for m in range(M):
                                for t in range(TILES):
                                    c = t * 256 + m * P
                                    op = nc.tensor.transpose(d_ps[q][:, m, t * P:(t + 1) * P],
                                                             gath[q][:, c:c + P], ident[:, :])
                            op.then_inc(s_dt, 1)
                        if on[3]:
                            pe.wait_ge(s_dh, done(G - 3))
                            pe.wait_ge(s_dl, done(G - 3))
                            pe.wait_ge(s_res, free(G - 3))
                            for m in range(M):
                                d = slice(m * P, (m + 1) * P)
                                op = three(o_ps[1 - q][:, m],
                                           [((wmh[:, k, d], wml[:, k, d]), (xh[:, 1 - q, k], xl[:, 1 - q, k]))
                                            for k in range(M)])
                            op.then_inc(s_o, 1)

                    pipeline(pe, step_b)

                regions(pe, n, region)

                pe.wait_ge(s_st1, n + 1)
                mm(n_ps[:, 0:4], gsum[:, :], small[:, 58:62], start=True, stop=True).then_inc(s_gst1, 1)
                pe.wait_ge(s_y1, n + 1)
                for k in range(K):
                    op = mm(n_ps[0:HIDDEN, 8:9], w1s[:, k, :], small[:, 36 + k:37 + k], start=k == 0, stop=k == K - 1)
                op.then_inc(s_h1, 1)
                pe.wait_ge(s_h1r, n + 1)
                for m in range(M):
                    op = mm(n_ps[:, m:m + 1], w2s[:, m * P:(m + 1) * P], small[0:HIDDEN, 40:41], start=True, stop=True)
                op.then_inc(s_gz, 1)

            images(pe, image)


def kernel(**inputs):
    import numpy as _np
    import concourse.bacc as _bacc
    from concourse import mybir as _mybir
    from concourse.bass_utils import run_bass_kernel_spmd as _run

    a = {k: _np.asarray(v) for k, v in inputs.items()}
    C = a["x"].shape[1]
    wp = a["L0_conv_Wp"].reshape(HEADS, 2, CH, C)
    bp = a["L0_conv_bp"].reshape(HEADS, 2, CH)
    bv = bp[:, 1, :].reshape(HEADS // 2, 2, CH).transpose(1, 0, 2)
    first = _np.zeros((P, 1), _np.float32)
    first[::CENTRES] = 1.0
    arrays = {
        "x": a["x"],
        "wp_t": wp.transpose(3, 1, 0, 2).reshape(C, 2 * C),
        "bp_col": bp[:, 0, :].reshape(2, P).T,
        "bv_diag": _np.repeat(bv, CENTRES, axis=0),
        "wm_t": a["L0_conv_Wm"].T,
        "bm_col": a["L0_conv_bm"].reshape(2, P).T,
        "alpha": _np.repeat(a["L0_conv_alpha"].reshape(1, 1), P, axis=0),
        "beta": _np.repeat(a["L0_conv_beta"].reshape(1, 1), P, axis=0),
        "w1_t": a["L1_conv_w1"].T,
        "w2_t": a["L1_conv_w2"].T,
        "first_centre": first,
    }
    nc = _bacc.Bacc("TRN2", target_bir_lowering=False, num_devices=1)
    args = []
    for name in arrays:
        arrays[name] = _np.ascontiguousarray(arrays[name])
        args.append(nc.dram_tensor(name, arrays[name].shape, _mybir.dt.from_np(arrays[name].dtype),
                                   kind="ExternalInput").ap())
    args.append(nc.dram_tensor("out", a["x"].shape, _mybir.dt.from_np(a["x"].dtype), kind="ExternalOutput").ap())
    cluster_block(nc, *args)
    return _run(nc, [arrays], core_ids=[0]).results[0]["out"]
```
